# Optimizing a Trainium2 kernel written in Bass

```python
import numpy as np
import jax
import jax.numpy as jnp

def _softmax(x, axis=-1):
    return jax.nn.softmax(x, axis=axis)

def _gelu(x):
    return jax.nn.gelu(x, approximate=True)

def _silu(x):
    return jax.nn.silu(x)

def _sigmoid(x):
    return jax.nn.sigmoid(x)

def _layernorm(x, axis=-1, eps=1e-05):
    m = jnp.mean(x, axis=axis, keepdims=True)
    v = jnp.var(x, axis=axis, keepdims=True)
    return (x - m) / jnp.sqrt(v + eps)

def _scatter_add(tgt, idx, src, axis=0):
    return tgt.at[idx].add(src)

def _segment_sum(src, seg, n):
    return jax.ops.segment_sum(src, seg, n)
kernel_name = 'mk_seq_postln_d1_jaxref_r8_63142f'

def setup_inputs(seed: int=0):
    np.random.seed(seed)
    _w = jnp.asarray

    def _L0_attn_setup():
        import jax, jax.numpy as jnp
        import numpy as np
        import math
        N_HEAD = 16
        N_EMBD = 128
        HEAD_D = N_EMBD // N_HEAD
        BASE = 1250

        def rope(Y):
            d = Y.shape[-1]
            t = Y.shape[-2]
            theta = BASE ** (-2.0 * jnp.arange(d // 2, dtype=Y.dtype) / d)
            theta2 = jnp.concatenate([theta, theta], axis=0)
            pos = jnp.arange(1, t + 1, dtype=Y.dtype)
            C = pos[:, None] * theta2[None, :]
            cos, sin = (jnp.cos(C), jnp.sin(C))
            Y2 = jnp.concatenate([-Y[..., d // 2:], Y[..., :d // 2]], axis=-1)
            return Y * cos + Y2 * sin
        key = jax.random.key(seed)
        ks = jax.random.split(key, 9)
        s = 0.02
        x = jax.random.normal(ks[0], (4, 256, N_EMBD), dtype=jnp.float32)
        Wq = jax.random.normal(ks[1], (N_EMBD, N_EMBD), dtype=jnp.float32) * s
        bq = jnp.zeros((N_EMBD,), dtype=jnp.float32)
        Wk = jax.random.normal(ks[2], (N_EMBD, N_EMBD), dtype=jnp.float32) * s
        bk = jnp.zeros((N_EMBD,), dtype=jnp.float32)
        Wv = jax.random.normal(ks[3], (N_EMBD, N_EMBD), dtype=jnp.float32) * s
        bv = jnp.zeros((N_EMBD,), dtype=jnp.float32)
        Wo = jax.random.normal(ks[4], (N_EMBD, N_EMBD), dtype=jnp.float32) * s
        bo = jnp.zeros((N_EMBD,), dtype=jnp.float32)
        return {'x': x, 'Wq': Wq, 'bq': bq, 'Wk': Wk, 'bk': bk, 'Wv': Wv, 'bv': bv, 'Wo': Wo, 'bo': bo}
    _L0_attn_in = _L0_attn_setup()

    def _L0_ffn_setup():
        import jax, jax.numpy as jnp
        import numpy as np
        key = jax.random.key(seed)
        k1, k2, k3 = jax.random.split(key, 3)
        B, S, D, E, H = (4, 256, 128, 8, 128)
        x = jax.random.normal(k1, (B, S, D), dtype=jnp.float32)
        Wg = jax.random.normal(k2, (D, E), dtype=jnp.float32) / np.sqrt(D)
        We = jax.random.normal(k3, (E, D, H), dtype=jnp.float32) / np.sqrt(D)
        be = jnp.zeros((E, H), dtype=jnp.float32)
        return {'x': x, 'Wg': Wg, 'We': We, 'be': be}
    _L0_ffn_in = _L0_ffn_setup()
    _d = {'L0_attn_x': _L0_attn_in['x'], 'L0_attn_Wq': _L0_attn_in['Wq'], 'L0_attn_bq': _L0_attn_in['bq'], 'L0_attn_Wk': _L0_attn_in['Wk'], 'L0_attn_bk': _L0_attn_in['bk'], 'L0_attn_Wv': _L0_attn_in['Wv'], 'L0_attn_bv': _L0_attn_in['bv'], 'L0_attn_Wo': _L0_attn_in['Wo'], 'L0_attn_bo': _L0_attn_in['bo'], 'L0_ffn_Wg': _L0_ffn_in['Wg'], 'L0_ffn_We': _L0_ffn_in['We'], 'L0_ffn_be': _L0_ffn_in['be']}
    _x0 = _d['L0_attn_x']
    _d['L0_attn_x'] = jax.random.normal(jax.random.fold_in(jax.random.key(seed), 1), (16, 512, 128), dtype=_x0.dtype)
    del _x0
    return _d

def reference(L0_attn_x, L0_attn_Wq, L0_attn_bq, L0_attn_Wk, L0_attn_bk, L0_attn_Wv, L0_attn_bv, L0_attn_Wo, L0_attn_bo, L0_ffn_Wg, L0_ffn_We, L0_ffn_be):

    def _L0_attn_ref(x, Wq, bq, Wk, bk, Wv, bv, Wo, bo):
        import jax, jax.numpy as jnp
        import numpy as np
        import math
        N_HEAD = 16
        N_EMBD = 128
        HEAD_D = N_EMBD // N_HEAD
        BASE = 1250

        def rope(Y):
            d = Y.shape[-1]
            t = Y.shape[-2]
            theta = BASE ** (-2.0 * jnp.arange(d // 2, dtype=Y.dtype) / d)
            theta2 = jnp.concatenate([theta, theta], axis=0)
            pos = jnp.arange(1, t + 1, dtype=Y.dtype)
            C = pos[:, None] * theta2[None, :]
            cos, sin = (jnp.cos(C), jnp.sin(C))
            Y2 = jnp.concatenate([-Y[..., d // 2:], Y[..., :d // 2]], axis=-1)
            return Y * cos + Y2 * sin
        b, t, _ = x.shape

        def split_heads(y):
            return y.reshape(b, t, N_HEAD, HEAD_D).transpose(0, 2, 1, 3)
        q = split_heads(x @ Wq.T + bq)
        k = split_heads(x @ Wk.T + bk)
        v = split_heads(x @ Wv.T + bv)
        q, k = (rope(q), rope(k))
        scale = math.sqrt(HEAD_D)
        att = jnp.einsum('bhqd,bhkd->bhqk', q, k) / scale
        mask = jnp.tril(jnp.ones((t, t), dtype=bool))
        att = jnp.where(mask, att, -jnp.inf)
        att = jax.nn.softmax(att, axis=-1)
        y = jnp.einsum('bhqk,bhkd->bhqd', att, v)
        y = y.transpose(0, 2, 1, 3).reshape(b, t, N_EMBD)
        return y @ Wo.T + bo

    def _L0_ffn_ref(x, Wg, We, be):
        import jax, jax.numpy as jnp
        import numpy as np
        B, S, D = x.shape
        E = Wg.shape[1]
        T = B * S
        xf = x.reshape(T, D)
        gates = jax.nn.softmax(xf @ Wg, axis=-1)
        top_g, top_i = jax.lax.top_k(gates, 2)
        top_g = top_g / jnp.sum(top_g, axis=-1, keepdims=True)
        tok = jnp.arange(T)
        dispatch = jnp.zeros((E, T), dtype=gates.dtype)
        for i in range(2):
            dispatch = dispatch.at[top_i[:, i], tok].add(top_g[:, i])
        y = jnp.einsum('td,edh->eth', xf, We) + be[:, None, :]
        out = jnp.einsum('et,eth->th', dispatch, y)
        return out.reshape(B, S, -1)
    x = L0_attn_x
    x = _layernorm(x + _L0_attn_ref(x, L0_attn_Wq, L0_attn_bq, L0_attn_Wk, L0_attn_bk, L0_attn_Wv, L0_attn_bv, L0_attn_Wo, L0_attn_bo), axis=-1)
    x = _layernorm(x + _L0_ffn_ref(x, L0_ffn_Wg, L0_ffn_We, L0_ffn_be), axis=-1)
    return x

_drawn_inputs = setup_inputs


def setup_inputs(seed=0):
    import zlib

    import numpy as np

    out = dict(_drawn_inputs(seed))
    spreads = {'L0_attn_bq': (0.0, 0.8),
     'L0_attn_bk': (0.0, 0.8),
     'L0_attn_bv': (0.0, 0.1),
     'L0_attn_bo': (0.0, 0.1),
     'L0_ffn_be': (0.0, 0.1)}
    factors = {'L0_attn_Wq': 8.0, 'L0_attn_Wk': 5.692}
    for name, (base, spread) in spreads.items():
        noise = np.random.default_rng([zlib.crc32(name.encode()), seed]).standard_normal(out[name].shape)
        drawn = base * np.exp(spread * noise) if base else spread * noise
        out[name] = jnp.asarray(drawn.astype(out[name].dtype))
    for name, factor in factors.items():
        out[name] = (out[name] * factor).astype(out[name].dtype)
    return out
```

```python
from contextlib import ExitStack

import numpy as np
import concourse.bass as bass
from concourse import mybir

ALU = mybir.AluOpType
ACT = mybir.ActivationFunctionType
AX = mybir.AxisListType
F32 = mybir.dt.float32
BF16 = mybir.dt.bfloat16

P = 128
B, T = 16, 512
H, DH = 16, 8
NT = T // P
HG = 4
NG = H // HG
E = 8
HALF = DH // 2
TERMS_Q = (0, 0, 0, 1, 1, 2)
TERMS_K = (0, 1, 2, 0, 1, 0)
MAXROW = 96
KS = 96
KST = MAXROW + 2
SU = 11
TU = 10
EPS = 1e-5
SCALE = float(DH) ** -0.5
LOOP_FIRST, LOOP_PAIRS = 4, 5
LAST = B + 2
MM_PER_EXPERT_TILE = E + 1


class Row:

    def __init__(self, n, reg=None):
        self.n, self.reg = n, reg

    def __add__(self, k):
        return Row(self.n + k, self.reg)

    def __sub__(self, k):
        return Row(self.n - k, self.reg)

    @property
    def parity(self):
        return self.n % 2

    @property
    def real(self):
        return self.reg is not None or 0 <= self.n < B


def count(per_row, row, plus):
    if row.reg is None:
        return max(0, min(per_row * row.n + plus, per_row * B))
    assert per_row * row.n + plus > 0
    return row.reg * (2 * per_row) + (per_row * row.n + plus)


def count_parity(per_row, row):
    if row.reg is None:
        return per_row * (min(row.n, B - 2 + row.parity) // 2 + 1)
    assert row.n >= 0
    return row.reg * per_row + per_row * (row.n // 2 + 1)


def rows_of(row, t_first, n):
    if row.reg is None:
        return bass.ds(row.n * T + t_first, n)
    return bass.ds(row.reg * (2 * T) + (row.n * T + t_first), n)


def pipeline(eng, iteration):
    for n in range(-1, LOOP_FIRST):
        iteration(Row(n))
    with eng.Fori(0, LOOP_PAIRS) as i:
        iteration(Row(LOOP_FIRST, i))
        iteration(Row(LOOP_FIRST + 1, i))
    for n in range(LOOP_FIRST + 2 * LOOP_PAIRS, LAST + 1):
        iteration(Row(n))


def group_real(row, g):
    return row.reg is not None or 0 <= NG * row.n + g < NG * B


def score_unit(u):
    if u < 4:
        return 3, (u,)
    if u < 8:
        return 2, (u - 4,)
    if u < 10:
        return 1, (2 * u - 16, 2 * u - 15)
    return 0, (0, 1, 2, 3)


def key_unit(u):
    if u < 4:
        return ((u, 0, 0),)
    if u < 8:
        return ((u - 4, 3, 0), (u - 4, 1, P))
    return ((2 * u - 16, 2, 0), (2 * u - 15, 2, 2 * P))


def key_place(hg, kb):
    return {0: (hg, 0), 1: (4 + hg, P), 3: (4 + hg, 0), 2: (8 + hg // 2, 2 * P * (hg % 2))}[kb]


def transformer_layer(nc, x, xT, wqT, wkT, wvT, woT, bq, bk, bv, bo, wg, we, be,
                      cos_t, sin_t, ident, identb, causal, ramp, out):
    with ExitStack() as ctx:
        def sb(name, shape, dt=F32):
            return ctx.enter_context(nc.sbuf_tensor(name, shape, dt))

        def bank(name):
            return ctx.enter_context(nc.psum_tensor(name, [P, T], F32))

        def sem(name):
            return ctx.enter_context(nc.semaphore(name))

        wq_s, wk_s, wv_s, wo_s = (sb(n, [P, P]) for n in ("wq_s", "wk_s", "wv_s", "wo_s"))
        bq_s, bk_s = sb("bq_s", [P, 1]), sb("bk_s", [P, 1])
        bv_s, bo_s = sb("bv_s", [P, P]), sb("bo_s", [P, P])
        wg_s = sb("wg_s", [P, 32])
        we_s = sb("we_s", [P, E, P])
        be_s = sb("be_s", [P, NT, P])
        cos_s, sin_s = sb("cos_s", [P, T]), sb("sin_s", [P, T])
        id_s, idb_s = sb("id_s", [P, P]), sb("idb_s", [P, P], BF16)
        causal_s = sb("causal_s", [P, P], BF16)
        ramp_s = sb("ramp_s", [P, NT, E])
        half_s = sb("half_s", [P, NT])

        xT_s = [sb(f"xT_s{i}", [P, T]) for i in range(2)]
        raw = {n: sb(n + "_raw", [P, T]) for n in "qk"}
        swap = {n: sb(n + "_swap", [P, T]) for n in "qk"}
        rot, rest = raw, swap
        parts = {n: sb(n + "_parts", [P, 3, T], BF16) for n in "qk"}
        qs = [sb(f"qs{i}", [P, H, T], BF16) for i in range(2)]
        ks = [sb(f"ks{i}", [P, H, T], BF16) for i in range(2)]
        vx = [sb(f"vx{i}", [P, NT, H, 32]) for i in range(2)]
        nmax = [sb(f"nmax{i}", [P, HG, NT]) for i in range(2)]
        nparts = [sb(f"nparts{i}", [P, 2, HG * NT], BF16) for i in range(2)]
        nrows = [sb(f"nrows{i}", [32, P], BF16) for i in range(2)]
        prob = sb("prob", [P, 2 * TU, T])
        ysum = [sb(f"ysum{i}", [P, T]) for i in range(2)]
        yT = [sb(f"yT{i}", [P, T]) for i in range(2)]
        den = [sb(f"den{i}", [P, T * H // P]) for i in range(2)]
        rden = [sb(f"rden{i}", [P, T * H // P]) for i in range(2)]
        rdenb = sb("rdenb", [P, T])
        yn = sb("yn", [P, T])
        x_s = [sb(f"x_s{i}", [P, NT, P]) for i in range(2)]
        xb = sb("xb", [P, NT, P])
        r1 = sb("r1", [P, NT, P])
        st1, mv1, ve1, rs1 = sb("st1", [P, NT, 6]), sb("mv1", [P, NT, 2]), sb("ve1", [P, NT]), sb("rs1", [P, NT])
        r2 = sb("r2", [P, NT, P])
        st2, mv2, ve2, rs2 = sb("st2", [P, NT, 6]), sb("mv2", [P, NT, 2]), sb("ve2", [P, NT]), sb("rs2", [P, NT])
        x1 = [sb(f"x1_{i}", [P, NT, P]) for i in range(2)]
        x1T = sb("x1T", [P, T])
        lg = sb("lg", [P, NT, 32])
        gv = [sb(f"gv{i}", [P, NT, 1]) for i in range(8)]
        gw = [sb(f"gw{i}", [P, NT, E]) for i in range(10)]
        wtok = sb("wtok", [P, NT, 32])
        wT = sb("wT", [P, P])
        wb = sb("wb", [P, E, T])
        xs = wb
        x2 = sb("x2", [P, NT, P])
        rden_dram = [nc.dram_tensor(f"rden_dram{i}", [H, T], F32, kind="Internal").ap() for i in range(2)]
        w_dram = [nc.dram_tensor(f"w_dram{i}", [E, T], F32, kind="Internal").ap() for i in range(2)]

        S = [bank("S0"), bank("S1")]
        ST = [bank("ST0"), bank("ST1")]
        PV = bank("PV")
        MO = bank("MO")
        X = [bank("X0"), bank("X1")]

        const_loaded = sem("const_loaded")
        const_set = sem("const_set")
        xT_loaded = [sem("xT_loaded0"), sem("xT_loaded1")]
        x_loaded = [sem("x_loaded0"), sem("x_loaded1")]
        proj_ready = sem("proj_ready")
        raw_ready = sem("raw_ready")
        swapped = {n: sem("swapped_" + n) for n in "qk"}
        rope_step = {n: sem("rope_step_" + n) for n in "qk"}
        hi_ready = {n: sem("hi_ready_" + n) for n in "qk"}
        mid_ready = {n: sem("mid_ready_" + n) for n in "qk"}
        stacked = {n: [sem(f"stacked_{n}{i}") for i in range(2)] for n in "qk"}
        v_ready, v_evac = sem("v_ready"), sem("v_evac")
        s_ready, max_done = sem("s_ready"), sem("max_done")
        nhi_ready, nparts_ready = sem("nhi_ready"), sem("nparts_ready")
        nT_ready, nT_evac = sem("nT_ready"), sem("nT_evac")
        nrow_stacked = [sem("nrow_stacked0"), sem("nrow_stacked1")]
        st_ready, exp_done = sem("st_ready"), sem("exp_done")
        masked, pv_done, y_evac = sem("masked"), sem("pv_done"), sem("y_evac")
        y_moved = [sem(f"y_moved{g}") for g in range(NG)]
        den_moved = [sem(f"den_moved{g}") for g in range(NG)]
        rden_ready, rden_stored, rdenb_loaded = sem("rden_ready"), sem("rden_stored"), sem("rdenb_loaded")
        yn_ready, xb_ready, o_ready = sem("yn_ready"), sem("xb_ready"), sem("o_ready")
        ln1_step, rs1_step, x1_ready = sem("ln1_step"), sem("rs1_step"), sem("x1_ready")
        x1T_ready, x1T_evac, lg_ready = sem("x1T_ready"), sem("x1T_evac"), sem("lg_ready")
        gate_step, p2_ready = sem("gate_step"), sem("p2_ready")
        w_stored, wb_loaded = sem("w_stored"), sem("wb_loaded")
        xs_dve, xs_pool, mo_ready = sem("xs_dve"), sem("xs_pool"), sem("mo_ready")
        ln2_step, rs2_step, x2_ready = sem("ln2_step"), sem("rs2_step"), sem("x2_ready")
        stored = sem("stored")
        half_set = sem("half_set")
        held = {e: sem("held_" + e) for e in ("dve", "pool", "sp")}

        block = ctx.enter_context(nc.Block())

        consts = [(wq_s[:], wqT), (bq_s[:], bq), (wk_s[:], wkT), (bk_s[:], bk), (cos_s[:], cos_t), (sin_s[:], sin_t),
                  (wv_s[:], wvT), (bv_s[:], bv.to_broadcast((P, P))), (idb_s[:], identb), (causal_s[:], causal),
                  (wo_s[:], woT), (bo_s[:], bo.to_broadcast((P, P))), (id_s[:], ident), (ramp_s[:], ramp),
                  (wg_s[:, 0:E], wg), (we_s[:], we)]
        consts += [(be_s[32 * c:32 * c + E, c, :], be) for c in range(NT)]
        CONST = 16 * len(consts)
        MEMSETS = 11

        @block.sync
        def _(sp):
            sp.dma_start(xT_s[0][:], xT[:, 0:T]).then_inc(xT_loaded[0], 16)
            sp.wait_ge(const_set, MEMSETS)
            for dst, src in consts:
                sp.dma_start(dst, src).then_inc(const_loaded, 16)

            def swap_halves(n, row):
                sp.wait_ge(raw_ready, count(2, row, 1 + "qk".index(n)))
                sp.sem_inc(held["sp"])
                sp.wait_ge(rope_step[n], count(5, row, 0))
                sp.sem_inc(held["sp"])
                sp.dma_start(swap[n][0:64, :], raw[n][64:P, :]).then_inc(swapped[n], 16)
                sp.dma_start(swap[n][64:P, :], raw[n][0:64, :]).then_inc(swapped[n], 16)

            def stack(n, row):
                sp.wait_ge(rope_step[n], count(5, row, 5))
                sp.sem_inc(held["sp"])
                sp.wait_ge(mid_ready[n], count(1, row, 1))
                sp.sem_inc(held["sp"])
                sp.wait_ge(st_ready, count(NG * TU, row - 1, 0))
                sp.sem_inc(held["sp"])
                dst = (qs if n == "q" else ks)[row.parity]
                for t, part in enumerate(TERMS_Q if n == "q" else TERMS_K):
                    sp.dma_start(dst[DH * t:DH * (t + 1), :, :],
                                 parts[n][:, part, :]
                                 ).then_inc(stacked[n][row.parity], 16)

            def iteration(b):
                for g in range(NG):
                    if group_real(b, g - 4):
                        sp.wait_ge(y_evac, count(NG, b, g - 3))
                        sp.sem_inc(held["sp"])
                        row = b - 1
                        if g == 0:
                            sp.wait_ge(yn_ready, count(1, row, -1))
                            sp.sem_inc(held["sp"])
                            sp.wait_ge(rden_ready, count(1, row, -1))
                            sp.sem_inc(held["sp"])
                        for hg in range(HG):
                            at = 32 * g + DH * hg
                            sp.dma_start(yT[row.parity][at:at + DH, :], ysum[g % 2][32 * hg:32 * hg + DH, :]
                                         ).then_inc(y_moved[g], 16)
                        sp.dma_start(den[row.parity][32 * g:32 * g + 32, :], ysum[g % 2][DH:P:32, :]
                                     ).then_inc(den_moved[g], 16)
                    if g == 0:
                        if (b - 2).real:
                            row = b - 2
                            sp.wait_ge(rden_ready, count(1, row, 1))
                            sp.sem_inc(held["sp"])
                            sp.dma_start(rden_dram[row.parity].rearrange("h (a c) -> (h a) c", a=DH),
                                         rden[row.parity][:]).then_inc(rden_stored, 16)
                        if (b + 2).real:
                            row = b + 2
                            sp.wait_ge(v_ready, count(1, row, -1))
                            sp.sem_inc(held["sp"])
                            sp.dma_start(xT_s[row.parity][:], xT[:, rows_of(row, 0, T)]
                                         ).then_inc(xT_loaded[row.parity], 16)
                        elif b.n == -1:
                            sp.dma_start(xT_s[1][:], xT[:, T:2 * T]).then_inc(xT_loaded[1], 16)
                        if (b - 1).real:
                            row = b - 1
                            sp.wait_ge(xb_ready, count(1, row, -1))
                            sp.sem_inc(held["sp"])
                            sp.dma_start(x_s[row.parity][:],
                                         x[rows_of(row, 0, T), :].rearrange("(c p) d -> p c d", p=P)
                                         ).then_inc(x_loaded[row.parity], 16)
                        if (b + 1).real:
                            swap_halves("q", b + 1)
                        if (b - 2).real:
                            row = b - 2
                            sp.wait_ge(rden_stored, count(16, row, 16))
                            sp.sem_inc(held["sp"])
                            sp.wait_ge(yn_ready, count(1, row, 0))
                            sp.sem_inc(held["sp"])
                            sp.dma_start(rdenb[:], rden_dram[row.parity].unsqueeze(1).to_broadcast((H, DH, T))
                                         ).then_inc(rdenb_loaded, 16)
                    if g == 2 and (b + 1).real:
                        stack("q", b + 1)
                    if g == 3 and (b - 2).real:
                        row = b - 2
                        sp.wait_ge(gate_step, count(GATE, row, GATE))
                        sp.sem_inc(held["sp"])
                        for c in range(NT):
                            sp.dma_start(w_dram[row.parity][:, P * c:P * (c + 1)], wT[32 * c:32 * c + E, :]
                                         ).then_inc(w_stored, 16)
                        sp.wait_ge(w_stored, count(64, row, 64))
                        sp.sem_inc(held["sp"])
                        sp.wait_ge(mo_ready, count(1, row, 0))
                        sp.sem_inc(held["sp"])
                        sp.dma_start(wb[:], w_dram[row.parity].unsqueeze(0).to_broadcast((P, E, T))
                                     ).then_inc(wb_loaded, 16)
                    if group_real(b, g - 1):
                        sp.wait_ge(nT_evac, count(NG, b, g))
                        sp.sem_inc(held["sp"])
                        row = b if g >= 1 else b - 1
                        h0 = HG * ((g - 1) % NG)
                        sp.dma_start(qs[row.parity][MAXROW:MAXROW + 2, h0:h0 + HG, :], nrows[(g - 1) % 2][:]
                                     ).then_inc(nrow_stacked[(g - 1) % 2], 16)
                    if g == 0 and (b + 1).real:
                        swap_halves("k", b + 1)
                    if g == 2:
                        if (b + 1).real:
                            stack("k", b + 1)
                        if (b - 3).real:
                            row = b - 3
                            sp.wait_ge(x2_ready, count(1, row, 1))
                            sp.sem_inc(held["sp"])
                            sp.dma_start(out[rows_of(row, 0, T), :].rearrange("(c p) d -> p c d", p=P),
                                         x2[:]).then_inc(stored, 16)

            pipeline(sp, iteration)
            sp.wait_ge(stored, 16 * B)
            sp.wait_ge(rden_stored, 16 * B)
            sp.wait_ge(w_stored, 64 * B)

        @block.tensor
        def _(pe):
            def project(n, row):
                pe.wait_ge(xT_loaded[row.parity], count_parity(16, row))
                if n == "q":
                    pe.wait_ge(nT_evac, count(NG, row, -NG - 1))
                    pe.wait_ge(raw_ready, count(2, row, 0))
                else:
                    pe.wait_ge(raw_ready, count(2, row, 1))
                nc.tensor.matmul(X[0][:], (wq_s if n == "q" else wk_s)[:], xT_s[row.parity][:],
                                 start=True, stop=True).then_inc(proj_ready, 1)

            def project_v(row):
                pe.wait_ge(nT_evac, count(NG, row, -NG + 2))
                for t in range(NT):
                    mm = nc.tensor.matmul(X[1][:, P * t:P * (t + 1)], xT_s[row.parity][:, P * t:P * (t + 1)],
                                          wv_s[:], start=True, stop=True)
                mm.then_inc(v_ready, 1)

            def max_rows(b, g):
                dst = X[(1, 0, 1, 0)[g]]
                pe.wait_ge(nparts_ready, count(NG, b, g))
                pe.wait_ge(nT_evac, count(NG, b, g - 1))
                if g == 0:
                    pe.wait_ge(v_evac, count(1, b, 1))
                if g == 1:
                    pe.wait_ge(raw_ready, count(2, b + 1, 2))
                if g == 2:
                    pe.wait_ge(x1T_evac, count(1, b - 2, 1))
                if g == 3:
                    pe.wait_ge(gate_step, count(GATE, b - 2, 1))
                nc.tensor.transpose(dst[0:32, 0:P // 2].bitcast(BF16),
                                    nparts[(g - 1) % 2][:].rearrange("p r n -> p (r n)"),
                                    idb_s[:]).then_inc(nT_ready, 1)

            def scores(b, g, u):
                if g == 0 and u == 0:
                    pe.wait_ge(stacked["q"][b.parity], count_parity(96, b))
                    pe.wait_ge(stacked["k"][b.parity], count_parity(96, b))
                qt, heads = score_unit(u)
                dst = S[(SU * g + u) % 2]
                pe.wait_ge(max_done, count(NG * SU, b, SU * g + u - 1))
                n = P * (qt + 1)
                for j, hg in enumerate(heads):
                    h, at = HG * g + hg, n * j
                    nc.tensor.matmul(dst[:, at:at + n], qs[b.parity][0:KS, h, P * qt:P * (qt + 1)],
                                     ks[b.parity][0:KS, h, 0:n], start=True, stop=False)
                    mm = nc.tensor.matmul(dst[:, at + n - P:at + n], idb_s[:], causal_s[:],
                                          start=False, stop=True)
                mm.then_inc(s_ready, 1)

            def key_scores(b, g, u):
                row, gg = (b, g - 2) if g >= 2 else (b - 1, g + 2)
                if u == 0:
                    pair = 16 * 2 * b.n + 16 * ((g - 2) // 2 + 1)
                    if b.reg is None:
                        pe.wait_ge(nrow_stacked[g % 2], pair)
                    else:
                        pe.wait_ge(nrow_stacked[g % 2], b.reg * 64 + pair)
                pe.wait_ge(exp_done, count(NG * TU, row, TU * gg + u - 1))
                for hg, kb, at in key_unit(u):
                    h, n = HG * gg + hg, T - P * kb
                    mm = nc.tensor.matmul(ST[u % 2][:, at:at + n],
                                          ks[row.parity][0:KST, h, P * kb:P * (kb + 1)],
                                          qs[row.parity][0:KST, h, P * kb:T], start=True, stop=True)
                mm.then_inc(st_ready, 1)

            def values(b, g, kb):
                row, gg = (b, 0) if g == 3 else (b - 1, g + 1)
                if kb == 0:
                    pe.wait_ge(y_evac, count(NG, row, gg))
                    pe.wait_ge(v_evac, count(1, row, 1))
                pe.wait_ge(masked, count(4 * NG, row, 4 * gg + (1, 3, 4, 4)[kb]))
                for hg in range(HG):
                    unit, at = key_place(hg, kb)
                    mm = nc.tensor.matmul(PV[32 * hg:32 * hg + 32, P * kb:T], vx[row.parity][:, kb, HG * gg + hg, :],
                                          prob[:, TU * (gg % 2) + unit, at:at + T - P * kb],
                                          start=(kb == 0), stop=(kb == NT - 1))
                mm.then_inc(pv_done, 1)

            def output(row):
                b = row + 2
                pe.wait_ge(yn_ready, count(1, row, 1))
                pe.wait_ge(nT_evac, count(NG, b, 0))
                pe.wait_ge(v_evac, count(1, b, 1))
                pe.wait_ge(x1T_evac, count(1, row, 0))
                for t in range(NT):
                    mm = nc.tensor.matmul(X[1][:, P * t:P * (t + 1)], yn[:, P * t:P * (t + 1)], wo_s[:],
                                          start=True, stop=True)
                mm.then_inc(o_ready, 1)

            def transpose_x1(row):
                pe.wait_ge(x1_ready, count(1, row, 1))
                for t in range(NT):
                    mm = nc.tensor.transpose(X[1][:, P * t:P * (t + 1)], x1[row.parity][:, t, :], id_s[:])
                mm.then_inc(x1T_ready, 1)

            def logits(row):
                b = row + 2
                pe.wait_ge(x1T_evac, count(1, row, 1))
                pe.wait_ge(nT_evac, count(NG, b, 1))
                pe.wait_ge(raw_ready, count(2, b + 1, 2))
                pe.wait_ge(gate_step, count(GATE, row - 1, 1))
                for c in range(NT):
                    mm = nc.tensor.matmul(X[0][32 * c:32 * c + 32, 0:P], wg_s[:], x1T[:, P * c:P * (c + 1)],
                                          start=True, stop=True)
                mm.then_inc(lg_ready, 1)

            def experts(row, k):
                c, e = divmod(k, MM_PER_EXPERT_TILE)
                if k == 0:
                    pe.wait_ge(xs_dve, count(1, row, 1))
                    pe.wait_ge(xs_pool, count(1, row, 1))
                    pe.wait_ge(ln2_step, count(LN, row, -LN + 1))
                dst = MO[:, P * c:P * (c + 1)]
                if e < E:
                    mm = nc.tensor.matmul(dst, xs[:, e, P * c:P * (c + 1)], we_s[:, e, :], start=(e == 0), stop=False)
                else:
                    mm = nc.tensor.matmul(dst, wT[:], be_s[:, c, :], start=False, stop=True)
                if k == NT * MM_PER_EXPERT_TILE - 1:
                    mm.then_inc(mo_ready, 1)

            def iteration(b):
                k = 0
                for g in range(NG):
                    for u in range(SU):
                        if g == 0 and u == 0 and (b + 1).real:
                            project("q", b + 1)
                        if g == 2 and u == 0 and (b - 2).real:
                            logits(b - 2)
                        if b.real:
                            scores(b, g, u)
                        if u < TU and group_real(b, g - 2):
                            key_scores(b, g, u)
                        if u == 3 and group_real(b, g - 1):
                            max_rows(b, g)
                        if u in (1, 4, 6, 8) and group_real(b, g - 3):
                            values(b, g, (1, 4, 6, 8).index(u))
                        if g == 0 and u == 5 and (b + 1).real:
                            project("k", b + 1)
                        if g == 0 and u == 7 and (b - 2).real:
                            output(b - 2)
                        if g == 1 and u == 5 and (b - 2).real:
                            transpose_x1(b - 2)
                        if g == 3 and u == 5 and (b + 1).real:
                            project_v(b + 1)
                        if (g, u) in EXPERT_SLOTS and (b - 3).real:
                            for _ in range(EXPERT_MM):
                                if k < NT * MM_PER_EXPERT_TILE:
                                    experts(b - 3, k)
                                    k += 1

            pe.wait_ge(const_loaded, CONST)
            pe.wait_ge(const_set, MEMSETS)
            pipeline(pe, iteration)

        @block.scalar
        def _(act):
            def evac_raw(n, row):
                act.wait_ge(proj_ready, count(2, row, 1 + "qk".index(n)))
                act.wait_ge(rope_step[n], count(5, row, 0))
                act.wait_ge(swapped[n], count(32, row, 0))
                nc.scalar.activation(raw[n][:], X[0][:], ACT.Identity,
                                     bias=(bq_s if n == "q" else bk_s)[:, 0:1]).then_inc(raw_ready, 1)

            def part_hi(n, row):
                act.wait_ge(rope_step[n], count(5, row, 3))
                act.wait_ge(stacked[n][(row - 1).parity], count_parity(96, row - 1))
                nc.scalar.copy(parts[n][:, 0, :], rot[n][:]).then_inc(hi_ready[n], 1)

            def part_mid(n, row):
                act.wait_ge(rope_step[n], count(5, row, 4))
                nc.scalar.copy(parts[n][:, 1, :], rest[n][:]).then_inc(mid_ready[n], 1)

            def exponent(b, g, u):
                row, gg = (b, g - 2) if g >= 2 else (b - 1, g + 2)
                if u == 0:
                    act.wait_ge(pv_done, count(4 * NG, row, 4 * (gg - 1)))
                act.wait_ge(st_ready, count(NG * TU, row, TU * gg + u + 1))
                nc.scalar.activation(prob[:, TU * (gg % 2) + u, :], ST[u % 2][:], ACT.Exp,
                                     scale=SCALE).then_inc(exp_done, 1)

            def evac_max_rows(b, g):
                act.wait_ge(nT_ready, count(NG, b, g))
                if group_real(b, g - 3):
                    value = 16 * 2 * b.n + 16 * ((g - 3) // 2 + 1)
                    act.wait_ge(nrow_stacked[(g - 1) % 2], value if b.reg is None else b.reg * 64 + value)
                nc.scalar.copy(nrows[(g - 1) % 2][:], X[(1, 0, 1, 0)[g]][0:32, 0:P // 2].bitcast(BF16)
                               ).then_inc(nT_evac, 1)

            def evac_y(b, g):
                row, gg = (b, 0) if g == 3 else (b - 1, g + 1)
                act.wait_ge(pv_done, count(4 * NG, row, 4 * gg + 4))
                if group_real(row, gg - 2):
                    old = row if gg >= 2 else row - 1
                    act.wait_ge(y_moved[(gg - 2) % NG], count(16 * HG, old, 16 * HG))
                    act.wait_ge(den_moved[(gg - 2) % NG], count(16, old, 16))
                nc.scalar.copy(ysum[gg % 2][:], PV[:]).then_inc(y_evac, 1)

            def iteration(b):
                for g in range(NG):
                    for u in range(SU):
                        if u < TU and group_real(b, g - 2):
                            exponent(b, g, u)
                        if u == 5 and group_real(b, g - 1):
                            evac_max_rows(b, g)
                        if u == 10 and group_real(b, g - 3):
                            evac_y(b, g)
                        if (b + 1).real:
                            if (g, u) == (0, 1):
                                evac_raw("q", b + 1)
                            if (g, u) == (0, 6):
                                evac_raw("k", b + 1)
                            if (g, u) == (0, 9):
                                part_hi("q", b + 1)
                            if (g, u) == (1, 4):
                                part_mid("q", b + 1)
                            if (g, u) == (1, 8):
                                part_hi("k", b + 1)
                            if (g, u) == (2, 3):
                                part_mid("k", b + 1)
                        if (b - 2).real:
                            if (g, u) == (1, 7):
                                act.wait_ge(x1T_ready, count(1, b - 2, 1))
                                act.wait_ge(xs_dve, count(1, b - 2, 0))
                                act.wait_ge(xs_pool, count(1, b - 2, 0))
                                nc.scalar.copy(x1T[:], X[1][:]).then_inc(x1T_evac, 1)
                            if (g, u) == (2, 6):
                                act.wait_ge(gate_step, count(GATE, b - 2, 8))
                                nc.scalar.activation(gv[3][:], gv[2][:], ACT.Exp).then_inc(p2_ready, 1)

            act.wait_ge(const_loaded, CONST)
            pipeline(act, iteration)

        @block.vector
        def _(dve):
            def reduce_scores(b, g, u):
                qt, heads = score_unit(u)
                n = P * (qt + 1)
                dve.wait_ge(s_ready, count(NG * SU, b, SU * g + u + 1))
                nc.vector.tensor_reduce(nmax[g % 2][:, heads[0]:heads[-1] + 1, qt],
                                        S[(SU * g + u) % 2][:, 0:n * len(heads)].rearrange("p (h n) -> p h n", n=n),
                                        AX.X, ALU.max, negate=True).then_inc(max_done, 1)

            def split_max(b, g):
                dve.wait_ge(max_done, count(NG * SU, b, SU * (g + 1)))
                dve.wait_ge(nT_ready, count(NG, b, g - 1))
                m = nmax[g % 2][:].rearrange("p h t -> p (h t)")
                nc.vector.tensor_copy(nparts[g % 2][:, 0, :], m).then_inc(nhi_ready, 1)
                dve.wait_ge(nhi_ready, count(NG, b, g + 1))
                nc.vector.tensor_tensor(nparts[g % 2][:, 1, :], m, nparts[g % 2][:, 0, :],
                                        ALU.subtract).then_inc(nparts_ready, 1)

            def evac_v(row):
                dve.wait_ge(v_ready, count(1, row, 1))
                dve.wait_ge(pv_done, count(4 * NG, row, -4 * NG))
                nc.vector.tensor_tensor(vx[row.parity][:, :, :, 0:DH],
                                        X[1][:].rearrange("p (t h d) -> p t h d", t=NT, h=H),
                                        bv_s[:].rearrange("p (h d) -> p h d", h=H).unsqueeze(1)
                                        .to_broadcast((P, NT, H, DH)), ALU.add).then_inc(v_evac, 1)

            def invert_sums(row):
                for moved in den_moved:
                    dve.wait_ge(moved, count(16, row, 16))
                dve.wait_ge(rden_stored, count(16, row, -16))
                nc.vector.reciprocal(rden[row.parity][:], den[row.parity][:]).then_inc(rden_ready, 1)

            def norm(row, step, base, src, other, r, st, mv, rs_step, rs, dst, done, guard):
                sem_ = base
                if step == 0:
                    guard()
                    nc.vector.tensor_tensor(r[:], src[:].rearrange("p (t d) -> p t d", t=NT), other[:],
                                            ALU.add).then_inc(sem_, 1)
                if step == 1:
                    dve.wait_ge(sem_, count(LN, row, 1))
                    for t in range(NT):
                        ins = nc.vector.bn_stats(st[:, t, :], r[:, t, :])
                    ins.then_inc(sem_, 1)
                if step == 2:
                    dve.wait_ge(sem_, count(LN, row, 2))
                    dve.wait_ge(rs_step, count(2, row, 0))
                    dve.sem_inc(held["dve"])
                    for t in range(NT):
                        ins = nc.vector.bn_aggr(mv[:, t, :], st[:, t, :])
                    ins.then_inc(sem_, 1)
                if step == 3:
                    dve.wait_ge(rs_step, count(2, row, 2))
                    dve.wait_ge(sem_, count(LN, row, 3))
                    for t in range(NT):
                        ins = nc.vector.tensor_scalar(dst[:, t, :], r[:, t, :], mv[:, t, 0:1], rs[:, t:t + 1],
                                                      ALU.subtract, ALU.mult)
                    ins.then_inc(done, 1)

            def norm1(row, step):
                def guard():
                    dve.wait_ge(o_ready, count(1, row, 1))
                    dve.wait_ge(xb_ready, count(1, row, 1))
                if step == 3:
                    dve.wait_ge(x1T_ready, count(1, row, -1))
                    dve.wait_ge(ln2_step, count(LN, row, -LN - LN + 1))
                norm(row, step, ln1_step, X[1], xb, r1, st1, mv1, rs1_step, rs1, x1[row.parity], x1_ready, guard)

            def norm2(row, step):
                def guard():
                    dve.wait_ge(mo_ready, count(1, row, 1))
                if step == 3:
                    dve.wait_ge(stored, count(16, row, 0))
                norm(row, step, ln2_step, MO, x1[row.parity], r2, st2, mv2, rs2_step, rs2, x2,
                     x2_ready, guard)

            def gates_a(row):
                dve.wait_ge(lg_ready, count(1, row, 1))
                nc.vector.transpose(lg[:].rearrange("p a e -> p (a e)"), X[0][:, 0:P]).then_inc(gate_step, 1)
                dve.wait_ge(gate_step, count(GATE, row, 1))
                nc.vector.tensor_reduce(m1_, lg[:, :, 0:E], AX.X, ALU.max).then_inc(gate_step, 1)
                dve.wait_ge(gate_step, count(GATE, row, 2))
                nc.vector.tensor_tensor(gw[0][:], lg[:, :, 0:E], gv[0][:].to_broadcast((P, NT, E)),
                                        ALU.subtract).then_inc(gate_step, 1)

            def gates_b(row):
                dve.wait_ge(gate_step, count(GATE, row, 3))
                nc.vector.scalar_tensor_tensor(out=gw[1][:], in0=gw[0][:], scalar=0.0, in1=ramp_s[:],
                                               op0=ALU.is_ge, op1=ALU.mult).then_inc(gate_step, 1)
                dve.wait_ge(gate_step, count(GATE, row, 4))
                nc.vector.tensor_reduce(gv[1][:].rearrange("p t o -> p (t o)"), gw[1][:], AX.X, ALU.max).then_inc(gate_step, 1)
                dve.wait_ge(gate_step, count(GATE, row, 5))
                nc.vector.tensor_tensor(gw[2][:], gw[1][:], gv[1][:].to_broadcast((P, NT, E)),
                                        ALU.is_equal).then_inc(gate_step, 1)

            def gates_c(row):
                dve.wait_ge(gate_step, count(GATE, row, 6))
                nc.vector.scalar_tensor_tensor(out=gw[3][:], in0=gw[2][:], scalar=-1e38, in1=gw[0][:],
                                               op0=ALU.mult, op1=ALU.add).then_inc(gate_step, 1)
                dve.wait_ge(gate_step, count(GATE, row, 7))
                dve.wait_ge(p2_ready, count(1, row, 0))
                nc.vector.tensor_reduce(gv[2][:].rearrange("p t o -> p (t o)"), gw[3][:], AX.X, ALU.max).then_inc(gate_step, 1)

            def gates_d(row):
                dve.wait_ge(gate_step, count(GATE, row, 8))
                nc.vector.tensor_tensor(gw[4][:], gw[3][:], gv[2][:].to_broadcast((P, NT, E)),
                                        ALU.is_equal).then_inc(gate_step, 1)
                dve.wait_ge(gate_step, count(GATE, row, 9))
                nc.vector.tensor_tensor(gw[5][:], gw[4][:], ramp_s[:], ALU.mult).then_inc(gate_step, 1)
                dve.wait_ge(gate_step, count(GATE, row, 10))
                nc.vector.tensor_reduce(gv[4][:].rearrange("p t o -> p (t o)"), gw[5][:], AX.X, ALU.max).then_inc(gate_step, 1)
                dve.wait_ge(gate_step, count(GATE, row, 11))
                nc.vector.tensor_tensor(gw[6][:], gw[5][:], gv[4][:].to_broadcast((P, NT, E)),
                                        ALU.is_equal).then_inc(gate_step, 1)

            def gates_e(row):
                dve.wait_ge(p2_ready, count(1, row, 1))
                nc.vector.tensor_scalar(gv[5][:], gv[3][:], 1.0, None, ALU.add).then_inc(gate_step, 1)
                dve.wait_ge(gate_step, count(GATE, row, 13))
                nc.vector.reciprocal(gv[6][:], gv[5][:]).then_inc(gate_step, 1)
                dve.wait_ge(gate_step, count(GATE, row, 14))
                nc.vector.tensor_tensor(gv[7][:], gv[3][:], gv[6][:], ALU.mult).then_inc(gate_step, 1)

            def gates_f(row):
                nc.vector.tensor_tensor(gw[7][:], gw[2][:], gv[6][:].to_broadcast((P, NT, E)),
                                        ALU.mult).then_inc(gate_step, 1)
                dve.wait_ge(gate_step, count(GATE, row, 15))
                nc.vector.tensor_tensor(gw[8][:], gw[6][:], gv[7][:].to_broadcast((P, NT, E)),
                                        ALU.mult).then_inc(gate_step, 1)
                dve.wait_ge(gate_step, count(GATE, row, 17))
                nc.vector.tensor_tensor(wtok[:, :, 0:E], gw[7][:], gw[8][:], ALU.add).then_inc(gate_step, 1)
                dve.wait_ge(gate_step, count(GATE, row, 18))
                dve.wait_ge(w_stored, count(64, row, 0))
                dve.wait_ge(mo_ready, count(1, row, 0))
                nc.vector.transpose(wT[:], wtok[:].rearrange("p a e -> p (a e)")).then_inc(gate_step, 1)

            m1_ = gv[0][:].rearrange("p t o -> p (t o)")

            def scale_x1(row):
                dve.wait_ge(wb_loaded, count(16, row, 16))
                dve.wait_ge(x1T_evac, count(1, row, 1))
                nc.vector.tensor_tensor(xs[:, 0:E_DVE, :], wb[:, 0:E_DVE, :],
                                        x1T[:].unsqueeze(1).to_broadcast((P, E_DVE, T)), ALU.mult
                                        ).then_inc(xs_dve, 1)

            def iteration(b):
                for g in range(NG):
                    for u in range(SU):
                        if b.real:
                            reduce_scores(b, g, u)
                            if u == SU - 1:
                                split_max(b, g)
                        at = (g, u)
                        if (b - 2).real:
                            if at == (0, 9):
                                norm1(b - 2, 0)
                            if at == (0, 10):
                                norm1(b - 2, 1)
                            if at == (1, 0):
                                norm1(b - 2, 2)
                            if at == (1, 2):
                                norm1(b - 2, 3)
                            if at == (2, 1):
                                gates_a(b - 2)
                            if at == (2, 2):
                                gates_b(b - 2)
                            if at == (2, 3):
                                gates_c(b - 2)
                            if at == (2, 5):
                                gates_d(b - 2)
                            if at == (2, 7):
                                gates_e(b - 2)
                            if at == (2, 8):
                                gates_f(b - 2)
                            if at == (3, 9):
                                scale_x1(b - 2)
                        if (b - 3).real:
                            if at == (1, 9):
                                norm2(b - 3, 0)
                            if at == (1, 10):
                                norm2(b - 3, 1)
                            if at == (2, 0):
                                norm2(b - 3, 2)
                            if at == (2, 4):
                                norm2(b - 3, 3)
                        if at == (3, 7) and (b + 1).real:
                            evac_v(b + 1)
                        if at == (3, 6) and (b - 1).real:
                            invert_sums(b - 1)

            nc.vector.memset(wg_s[:], 0.0).then_inc(const_set, 1)
            nc.vector.memset(be_s[:], 0.0).then_inc(const_set, 1)
            nc.vector.memset(wtok[:], 0.0).then_inc(const_set, 1)
            for i in range(2):
                nc.vector.memset(qs[i][0:KS, :, :], 0.0).then_inc(const_set, 1)
                nc.vector.memset(ks[i][0:KS, :, :], 0.0).then_inc(const_set, 1)
                nc.vector.memset(ks[i][MAXROW:KST, :, :], 1.0).then_inc(const_set, 1)
                nc.vector.memset(vx[i][:], 1.0).then_inc(const_set, 1)
            dve.wait_ge(const_loaded, CONST)
            dve.wait_ge(const_set, MEMSETS)
            pipeline(dve, iteration)

        @block.gpsimd
        def _(pool):
            G_ = nc.gpsimd

            def rope(n, row, step):
                s = rope_step[n]
                if step == 0:
                    pool.wait_ge(swapped[n], count(32, row, 32))
                    G_.tensor_tensor(rot[n][:], raw[n][:], cos_s[:], ALU.mult).then_inc(s, 1)
                if step == 1:
                    G_.tensor_tensor(rest[n][:], swap[n][:], sin_s[:], ALU.mult).then_inc(s, 1)
                if step == 2:
                    pool.wait_ge(s, count(5, row, 2))
                    G_.tensor_tensor(rot[n][:], rot[n][:], rest[n][:], ALU.add).then_inc(s, 1)
                if step == 3:
                    pool.wait_ge(s, count(5, row, 3))
                    pool.wait_ge(hi_ready[n], count(1, row, 1))
                    G_.tensor_tensor(rest[n][:], rot[n][:], parts[n][:, 0, :], ALU.subtract).then_inc(s, 1)
                if step == 4:
                    pool.wait_ge(s, count(5, row, 4))
                    pool.wait_ge(mid_ready[n], count(1, row, 1))
                    G_.tensor_tensor(parts[n][:, 2, :], rest[n][:], parts[n][:, 1, :], ALU.subtract).then_inc(s, 1)

            def mask(b, g, k):
                row, gg = (b, g - 2) if g >= 2 else (b - 1, g + 2)
                pool.wait_ge(exp_done, count(NG * TU, row, TU * gg + (4, 6, 8, 10)[k]))
                pool.sem_inc(held["pool"])
                s = TU * (gg % 2)
                if k == 0:
                    v, pattern = prob[:, s:s + 4, 0:P], [[0, 4], [1, P]]
                elif k < 3:
                    v = prob[:, s + 2 + 2 * k:s + 4 + 2 * k, 0:2 * P]
                    pattern = [[0, 2], [0, 2], [1, P]]
                else:
                    v = prob[:, s + 8:s + 10, :].rearrange("p u (c q) -> p (u c) q", q=2 * P)[:, :, 0:P]
                    pattern = [[0, 4], [1, P]]
                G_.affine_select(out=v, in_=v, compare_op=ALU.is_ge, fill=0.0, base=0, pattern=pattern,
                                 channel_multiplier=-1).then_inc(masked, 1)

            def inverse_root(row, ln_step, rs_step, mv, ve, rs, used):
                pool.wait_ge(ln_step, count(LN, row, 3))
                pool.wait_ge(used, count(1, row, 0))
                pool.sem_inc(held["pool"])
                G_.tensor_scalar(ve[:], mv[:, :, 1], EPS, None, ALU.add).then_inc(rs_step, 1)
                pool.wait_ge(rs_step, count(2, row, 1))
                G_.tensor_tensor(rs[:], ve[:], half_s[:], ALU.pow).then_inc(rs_step, 1)

            def iteration(b):
                for g in range(NG):
                    for k in range(4):
                        at = (g, k)
                        if (b - 2).real:
                            row = b - 2
                            if at == (0, 0):
                                pool.wait_ge(x_loaded[row.parity], count_parity(16, row))
                                pool.wait_ge(ln1_step, count(LN, row, -LN + 1))
                                G_.tensor_tensor(xb[:], x_s[row.parity][:],
                                                 bo_s[:].unsqueeze(1).to_broadcast((P, NT, P)), ALU.add
                                                 ).then_inc(xb_ready, 1)
                            if at == (0, 2):
                                for moved in y_moved:
                                    pool.wait_ge(moved, count(16 * HG, row, 16 * HG))
                                pool.wait_ge(rdenb_loaded, count(16, row, 16))
                                pool.wait_ge(o_ready, count(1, row, 0))
                                G_.tensor_tensor(yn[:], yT[row.parity][:], rdenb[:], ALU.mult).then_inc(yn_ready, 1)
                            if at == (1, 1):
                                inverse_root(row, ln1_step, rs1_step, mv1, ve1, rs1, x1_ready)
                        if (b - 3).real and at == (2, 1):
                            inverse_root(b - 3, ln2_step, rs2_step, mv2, ve2, rs2, x2_ready)
                        if (b + 1).real:
                            for when, n, step in ROPE_SLOTS:
                                if when == at:
                                    rope(n, b + 1, step)
                        if group_real(b, g - 2):
                            mask(b, g, k)
                if (b - 2).real:
                    row = b - 2
                    pool.wait_ge(wb_loaded, count(16, row, 16))
                    pool.wait_ge(x1T_evac, count(1, row, 1))
                    G_.tensor_tensor(xs[:, E_DVE:E, :], wb[:, E_DVE:E, :],
                                     x1T[:].unsqueeze(1).to_broadcast((P, E - E_DVE, T)), ALU.mult
                                     ).then_inc(xs_pool, 1)

            G_.memset(half_s[:], -0.5).then_inc(half_set, 1)
            pool.wait_ge(half_set, 1)
            pool.wait_ge(const_loaded, CONST)
            pipeline(pool, iteration)


GATE = 19
LN = 3
E_DVE = 5
EXPERT_SLOTS = [(0, u) for u in range(2, 11)] + [(1, u) for u in range(9)]
EXPERT_MM = 2
ROPE_SLOTS = [((0, 1), "q", 0), ((0, 2), "q", 1), ((0, 3), "q", 2), ((1, 0), "q", 3), ((1, 0), "k", 0),
              ((1, 1), "k", 1), ((1, 2), "k", 2), ((1, 3), "q", 4), ((2, 0), "k", 3), ((2, 2), "k", 4)]


def kernel(**inputs):
    import concourse.bacc as bacc
    from concourse.bass_utils import run_bass_kernel_spmd as run

    a = {k: np.ascontiguousarray(v) for k, v in inputs.items()}
    x = a["L0_attn_x"].reshape(B * T, P)
    order = np.arange(P).reshape(H, DH).T.reshape(-1)
    f = np.float32
    theta = np.power(f(1250), f(-2.0) * np.arange(HALF, dtype=f) / f(DH)).astype(f)
    angle = np.arange(1, T + 1, dtype=f)[:, None] * np.concatenate([theta, theta])[None, :]
    cos_t = np.repeat(np.cos(angle).T, H, axis=0).astype(f)
    sign = np.where(np.arange(DH) < HALF, -1, 1).astype(f)
    sin_t = np.repeat((np.sin(angle) * sign).T, H, axis=0).astype(f)
    bf = mybir.dt.np(BF16)
    q, k = np.arange(P)[:, None], np.arange(P)[None, :]
    arrays = {
        "x": x, "xT": x.T,
        "wqT": a["L0_attn_Wq"].T[:, order], "wkT": a["L0_attn_Wk"].T[:, order],
        "wvT": a["L0_attn_Wv"].T, "woT": a["L0_attn_Wo"].T,
        "bq": a["L0_attn_bq"][order].reshape(P, 1), "bk": a["L0_attn_bk"][order].reshape(P, 1),
        "bv": a["L0_attn_bv"].reshape(1, P), "bo": a["L0_attn_bo"].reshape(1, P),
        "wg": a["L0_ffn_Wg"], "we": a["L0_ffn_We"].transpose(1, 0, 2), "be": a["L0_ffn_be"],
        "cos_t": cos_t, "sin_t": sin_t,
        "ident": np.eye(P, dtype=f), "identb": np.eye(P).astype(bf),
        "causal": np.where(k > q, -3e38, 0).astype(bf),
        "ramp": np.broadcast_to(E - np.arange(E, dtype=f), (P, NT, E)),
    }
    nc = bacc.Bacc("TRN2", target_bir_lowering=False, num_devices=1)
    arrays = {n: np.ascontiguousarray(v) for n, v in arrays.items()}
    args = [nc.dram_tensor(n, v.shape, mybir.dt.from_np(v.dtype), kind="ExternalInput").ap() for n, v in arrays.items()]
    args.append(nc.dram_tensor("out", (B * T, P), F32, kind="ExternalOutput").ap())
    transformer_layer(nc, *args)
    r = run(nc, [arrays], core_ids=[0])
    return r.results[0]["out"].reshape(B, T, P)
```

```python
from contextlib import ExitStack

import numpy as np
import concourse.bass as bass
from concourse import mybir

ALU = mybir.AluOpType
ACT = mybir.ActivationFunctionType
AX = mybir.AxisListType
F32 = mybir.dt.float32
BF16 = mybir.dt.bfloat16

P = 128
B, T = 16, 512
H, DH = 16, 8
NT = T // P
HG = 4
NG = H // HG
E = 8
HALF = DH // 2
TERMS_Q = (0, 0, 0, 1, 1, 2)
TERMS_K = (0, 1, 2, 0, 1, 0)
MAXROW = 96
KS = 96
KST = MAXROW + 2
SU = 11
TU = 10
EH = E // 2
EPS = 1e-5
SCALE = float(DH) ** -0.5
LOOP_FIRST, LOOP_PAIRS = 4, 5
LAST = B + 2
EXPERT_PRODUCTS = 1 + NT * E


class Row:

    def __init__(self, n, reg=None):
        self.n, self.reg = n, reg

    def __add__(self, k):
        return Row(self.n + k, self.reg)

    def __sub__(self, k):
        return Row(self.n - k, self.reg)

    @property
    def parity(self):
        return self.n % 2

    @property
    def real(self):
        return self.reg is not None or 0 <= self.n < B


def count(per_row, row, plus):
    if row.reg is None:
        return max(0, min(per_row * row.n + plus, per_row * B))
    assert per_row * row.n + plus > 0
    return row.reg * (2 * per_row) + (per_row * row.n + plus)


def count_parity(per_row, row):
    if row.reg is None:
        return per_row * (min(row.n, B - 2 + row.parity) // 2 + 1)
    assert row.n >= 0
    return row.reg * per_row + per_row * (row.n // 2 + 1)


def rows_of(row, t_first, n):
    if row.reg is None:
        return bass.ds(row.n * T + t_first, n)
    return bass.ds(row.reg * (2 * T) + (row.n * T + t_first), n)


def pipeline(eng, iteration):
    for n in range(-1, LOOP_FIRST):
        iteration(Row(n))
    with eng.Fori(0, LOOP_PAIRS) as i:
        iteration(Row(LOOP_FIRST, i))
        iteration(Row(LOOP_FIRST + 1, i))
    for n in range(LOOP_FIRST + 2 * LOOP_PAIRS, LAST + 1):
        iteration(Row(n))


def ending(b):
    return b.reg is None and b.n > B


def group_real(row, g):
    return row.reg is not None or 0 <= NG * row.n + g < NG * B


def score_unit(u):
    if u < 4:
        return 3, (u,)
    if u < 8:
        return 2, (u - 4,)
    if u < 10:
        return 1, (2 * u - 16, 2 * u - 15)
    return 0, (0, 1, 2, 3)


def key_unit(u):
    if u < 4:
        return ((u, 0, 0),)
    if u < 8:
        return ((u - 4, 3, 0), (u - 4, 1, P))
    return ((2 * u - 16, 2, 0), (2 * u - 15, 2, 2 * P))


def key_place(hg, kb):
    return {0: (hg, 0), 1: (4 + hg, P), 3: (4 + hg, 0), 2: (8 + hg // 2, 2 * P * (hg % 2))}[kb]


def transformer_layer(nc, x, xT, qk_consts, rotation, consts, masks, bv, bo, we, be, out):
    with ExitStack() as ctx:
        def sb(name, shape, dt=F32):
            return ctx.enter_context(nc.sbuf_tensor(name, shape, dt))

        def bank(name):
            return ctx.enter_context(nc.psum_tensor(name, [P, T], F32))

        def sem(name):
            return ctx.enter_context(nc.semaphore(name))

        qk_s = sb("qk_s", [P, 2 * P + 2])
        wq_s, wk_s, bq_s, bk_s = qk_s[:, 0:P], qk_s[:, P:2 * P], qk_s[:, 2 * P:2 * P + 1], qk_s[:, 2 * P + 1:]
        rotation_s = sb("rotation_s", [P, 2, T])
        cos_s, sin_s = rotation_s[:, 0, :], rotation_s[:, 1, :]
        consts_s = sb("consts_s", [P, 3 * P + 32 + NT * E])
        wv_s, wo_s, id_s = (consts_s[:, P * i:P * (i + 1)] for i in range(3))
        wg_s = consts_s[:, 3 * P:3 * P + 32]
        ramp_s = consts_s[:, 3 * P + 32:].rearrange("p (t e) -> p t e", t=NT)
        masks_s = sb("masks_s", [P, 2 * P], BF16)
        idb_s, causal_s = masks_s[:, 0:P], masks_s[:, P:2 * P]
        bv_s, bo_s = sb("bv_s", [P, P]), sb("bo_s", [P, P])
        we_s = sb("we_s", [P, E, P])
        be_s = sb("be_s", [P, NT, P])
        half_s = sb("half_s", [P, NT])

        xT_s = [sb(f"xT_s{i}", [P, T]) for i in range(2)]
        raw = {n: sb(n + "_raw", [P, T]) for n in "qk"}
        swap = {n: sb(n + "_swap", [P, T]) for n in "qk"}
        rot, rest = raw, swap
        parts = {n: sb(n + "_parts", [P, 3, T], BF16) for n in "qk"}
        qs = [sb(f"qs{i}", [P, H, T], BF16) for i in range(2)]
        ks = [sb(f"ks{i}", [P, H, T], BF16) for i in range(2)]
        vx = [sb(f"vx{i}", [P, NT, H, 32]) for i in range(2)]
        nmax = [sb(f"nmax{i}", [P, HG, NT]) for i in range(2)]
        nparts = [sb(f"nparts{i}", [P, 2, HG * NT], BF16) for i in range(2)]
        nrows = [sb(f"nrows{i}", [32, P], BF16) for i in range(2)]
        prob = sb("prob", [P, 2 * TU, T])
        ysum = [sb(f"ysum{i}", [P, T]) for i in range(2)]
        yT = [sb(f"yT{i}", [P, T]) for i in range(2)]
        den = [sb(f"den{i}", [P, T * H // P]) for i in range(2)]
        rden = [sb(f"rden{i}", [P, T * H // P]) for i in range(2)]
        rdenb = sb("rdenb", [P, T])
        yn = sb("yn", [P, T])
        x_s = [sb(f"x_s{i}", [P, NT, P]) for i in range(2)]
        xb = sb("xb", [P, NT, P])
        r1 = sb("r1", [P, NT, P])
        st1, mv1, ve1, rs1 = sb("st1", [P, NT, 6]), sb("mv1", [P, NT, 2]), sb("ve1", [P, NT]), sb("rs1", [P, NT])
        r2 = sb("r2", [P, NT, P])
        st2, mv2, ve2, rs2 = sb("st2", [P, NT, 6]), sb("mv2", [P, NT, 2]), sb("ve2", [P, NT]), sb("rs2", [P, NT])
        x1 = [sb(f"x1_{i}", [P, NT, P]) for i in range(2)]
        x1T = sb("x1T", [P, T])
        lg = sb("lg", [P, NT, 32])
        gv = [sb(f"gv{i}", [P, NT, 1]) for i in range(8)]
        gw = [sb(f"gw{i}", [P, NT, E]) for i in range(10)]
        wtok = sb("wtok", [P, NT, 32])
        wT = [sb(f"wT{i}", [P, P]) for i in range(2)]
        wb = sb("wb", [P, E, T])
        xs = wb
        x2 = sb("x2", [P, NT, P])
        rden_dram = [nc.dram_tensor(f"rden_dram{i}", [H, T], F32, kind="Internal").ap() for i in range(2)]
        w_dram = [nc.dram_tensor(f"w_dram{i}", [E, T], F32, kind="Internal").ap() for i in range(2)]

        S = [bank("S0"), bank("S1")]
        ST = [bank("ST0"), bank("ST1")]
        PV = bank("PV")
        MO = bank("MO")
        X = [bank("X0"), bank("X1")]

        const_loaded = sem("const_loaded")
        qk_loaded = sem("qk_loaded")
        stack_set = [sem("stack_set0"), sem("stack_set1")]
        vx_set, wtok_set = sem("vx_set"), sem("wtok_set")
        xT_loaded = [sem("xT_loaded0"), sem("xT_loaded1")]
        x_loaded = [sem("x_loaded0"), sem("x_loaded1")]
        proj_ready = sem("proj_ready")
        raw_ready = sem("raw_ready")
        swapped = {n: sem("swapped_" + n) for n in "qk"}
        rope_step = {n: sem("rope_step_" + n) for n in "qk"}
        hi_ready = {n: sem("hi_ready_" + n) for n in "qk"}
        mid_ready = {n: sem("mid_ready_" + n) for n in "qk"}
        stacked = {n: [sem(f"stacked_{n}{i}") for i in range(2)] for n in "qk"}
        v_ready, v_evac = sem("v_ready"), sem("v_evac")
        s_ready, max_done = sem("s_ready"), sem("max_done")
        nhi_ready, nparts_ready = sem("nhi_ready"), sem("nparts_ready")
        nT_ready, nT_evac = sem("nT_ready"), sem("nT_evac")
        nrow_stacked = [sem("nrow_stacked0"), sem("nrow_stacked1")]
        st_ready, exp_done = sem("st_ready"), sem("exp_done")
        masked, pv_done, y_evac = sem("masked"), sem("pv_done"), sem("y_evac")
        y_moved = [sem(f"y_moved{g}") for g in range(NG)]
        den_moved = [sem(f"den_moved{g}") for g in range(NG)]
        rden_ready, rden_stored, rdenb_loaded = sem("rden_ready"), sem("rden_stored"), sem("rdenb_loaded")
        yn_ready, xb_ready, o_ready = sem("yn_ready"), sem("xb_ready"), sem("o_ready")
        ln1_step, rs1_step, x1_ready = sem("ln1_step"), sem("rs1_step"), sem("x1_ready")
        x1T_ready, x1T_evac, lg_ready = sem("x1T_ready"), sem("x1T_evac"), sem("lg_ready")
        gate_step, p2_ready = sem("gate_step"), sem("p2_ready")
        w_stored = sem("w_stored")
        wb_loaded = [sem(f"wb_loaded{i}") for i in range(2)]
        xs_dve, xs_pool, mo_ready = sem("xs_dve"), sem("xs_pool"), sem("mo_ready")
        ln2_step, rs2_step, x2_ready = sem("ln2_step"), sem("rs2_step"), sem("x2_ready")
        stored = sem("stored")
        half_set = sem("half_set")
        held = {e: sem("held_" + e) for e in ("dve", "pool", "sp")}

        block = ctx.enter_context(nc.Block())

        loads = [(rotation_s[:], rotation, qk_loaded), (masks_s[:], masks, const_loaded),
                 (consts_s[:], consts, const_loaded), (bv_s[:], bv.to_broadcast((P, P)), const_loaded),
                 (bo_s[:], bo.to_broadcast((P, P)), const_loaded), (we_s[:], we, const_loaded),
                 (be_s[:], be, const_loaded)]
        QK_CONST, CONST = 16 * 2, 16 * (len(loads) - 1)

        @block.sync
        def _(sp):
            sp.dma_start(xT_s[0][:], xT[:, 0:T]).then_inc(xT_loaded[0], 16)
            sp.dma_start(qk_s[:], qk_consts).then_inc(qk_loaded, 16)
            for dst, src, loaded in loads:
                sp.dma_start(dst, src).then_inc(loaded, 16)

            def swap_halves(n, row):
                sp.wait_ge(raw_ready, count(2, row, 1 + "qk".index(n)))
                sp.sem_inc(held["sp"])
                sp.wait_ge(rope_step[n], count(5, row, 0))
                sp.sem_inc(held["sp"])
                sp.dma_start(swap[n][0:64, :], raw[n][64:P, :]).then_inc(swapped[n], 16)
                sp.dma_start(swap[n][64:P, :], raw[n][0:64, :]).then_inc(swapped[n], 16)

            def stack(n, row):
                sp.wait_ge(st_ready, count(NG * TU, row - 1, 0))
                sp.sem_inc(held["sp"])
                if row.reg is None and row.n < 2:
                    sp.wait_ge(stack_set[row.parity], 2)
                dst = (qs if n == "q" else ks)[row.parity]
                for part in range(3):
                    if part == 0:
                        sp.wait_ge(hi_ready[n], count(1, row, 1))
                        sp.sem_inc(held["sp"])
                    if part == 1:
                        sp.wait_ge(mid_ready[n], count(1, row, 1))
                        sp.sem_inc(held["sp"])
                    if part == 2:
                        sp.wait_ge(rope_step[n], count(5, row, 5))
                        sp.sem_inc(held["sp"])
                    for t in range(len(TERMS_Q)):
                        if (TERMS_Q if n == "q" else TERMS_K)[t] == part:
                            sp.dma_start(dst[DH * t:DH * (t + 1), :, :], parts[n][:, part, :]
                                         ).then_inc(stacked[n][row.parity], 16)

            def load_weights(row, half):
                if half == 0:
                    sp.wait_ge(w_stored, count(64, row, 64))
                    sp.sem_inc(held["sp"])
                    sp.wait_ge(mo_ready, count(1, row, 0))
                    sp.sem_inc(held["sp"])
                sp.dma_start(wb[:, EH * half:EH * (half + 1), :],
                             w_dram[row.parity][EH * half:EH * (half + 1), :].unsqueeze(0).to_broadcast((P, EH, T))
                             ).then_inc(wb_loaded[half], 16)

            def spread_inverse_sums(row):
                sp.wait_ge(rden_ready, count(1, row, 1))
                sp.sem_inc(held["sp"])
                sp.dma_start(rden_dram[row.parity].rearrange("h (a c) -> (h a) c", a=DH),
                             rden[row.parity][:]).then_inc(rden_stored, 16)
                sp.wait_ge(rden_stored, count(16, row, 16))
                sp.sem_inc(held["sp"])
                sp.wait_ge(yn_ready, count(1, row, 0))
                sp.sem_inc(held["sp"])
                sp.dma_start(rdenb[:], rden_dram[row.parity].unsqueeze(1).to_broadcast((H, DH, T))
                             ).then_inc(rdenb_loaded, 16)

            def iteration(b):
                for g in range(NG):
                    if g == 0 and (b + 1).real:
                        swap_halves("q", b + 1)
                    if group_real(b, g - 4):
                        sp.wait_ge(y_evac, count(NG, b, g - 3))
                        sp.sem_inc(held["sp"])
                        row = b - 1
                        if g == 0:
                            sp.wait_ge(yn_ready, count(1, row, -1))
                            sp.sem_inc(held["sp"])
                            sp.wait_ge(rden_ready, count(1, row, -1))
                            sp.sem_inc(held["sp"])
                        sp.dma_start(den[row.parity][32 * g:32 * g + 32, :], ysum[g % 2][DH:P:32, :]
                                     ).then_inc(den_moved[g], 16)
                        for hg in range(HG):
                            at = 32 * g + DH * hg
                            sp.dma_start(yT[row.parity][at:at + DH, :], ysum[g % 2][32 * hg:32 * hg + DH, :]
                                         ).then_inc(y_moved[g], 16)
                    if g == 2 and (b + 1).real:
                        stack("q", b + 1)
                    if g == 3 and (b - 1).real and ending(b + 1):
                        spread_inverse_sums(b - 1)
                    if g == 3 and (b - 2).real:
                        row = b - 2
                        sp.wait_ge(gate_step, count(GATE, row, GATE))
                        sp.sem_inc(held["sp"])
                        for c in range(NT):
                            sp.dma_start(w_dram[row.parity][:, P * c:P * (c + 1)], wT[row.parity][32 * c:32 * c + E, :]
                                         ).then_inc(w_stored, 16)
                    if group_real(b, g - 1):
                        sp.wait_ge(nT_evac, count(NG, b, g))
                        sp.sem_inc(held["sp"])
                        row = b if g >= 1 else b - 1
                        h0 = HG * ((g - 1) % NG)
                        sp.dma_start(qs[row.parity][MAXROW:MAXROW + 2, h0:h0 + HG, :], nrows[(g - 1) % 2][:]
                                     ).then_inc(nrow_stacked[(g - 1) % 2], 16)
                    if g == 3 and (b - 2).real:
                        load_weights(b - 2, 0)
                    if g == 3 and (b - 1).real and not ending(b + 1):
                        spread_inverse_sums(b - 1)
                    if g == 3 and (b - 2).real:
                        load_weights(b - 2, 1)
                    if g == 0 and (b + 1).real:
                        swap_halves("k", b + 1)
                    if g == 0:
                        if (b + 2).real:
                            row = b + 2
                            sp.wait_ge(v_ready, count(1, row, -1))
                            sp.sem_inc(held["sp"])
                            sp.dma_start(xT_s[row.parity][:], xT[:, rows_of(row, 0, T)]
                                         ).then_inc(xT_loaded[row.parity], 16)
                        elif b.n == -1:
                            sp.dma_start(xT_s[1][:], xT[:, T:2 * T]).then_inc(xT_loaded[1], 16)
                        if (b - 1).real:
                            row = b - 1
                            sp.wait_ge(xb_ready, count(1, row, -1))
                            sp.sem_inc(held["sp"])
                            sp.dma_start(x_s[row.parity][:],
                                         x[rows_of(row, 0, T), :].rearrange("(c p) d -> p c d", p=P)
                                         ).then_inc(x_loaded[row.parity], 16)
                    if g == 2:
                        if (b + 1).real:
                            stack("k", b + 1)
                    if g == 3:
                        if (b - 3).real:
                            row = b - 3
                            sp.wait_ge(x2_ready, count(1, row, 1))
                            sp.sem_inc(held["sp"])
                            sp.dma_start(out[rows_of(row, 0, T), :].rearrange("(c p) d -> p c d", p=P),
                                         x2[:]).then_inc(stored, 16)

            pipeline(sp, iteration)
            sp.wait_ge(stored, 16 * B)
            sp.wait_ge(rden_stored, 16 * B)
            sp.wait_ge(w_stored, 64 * B)

        @block.tensor
        def _(pe):
            def project(n, row):
                pe.wait_ge(xT_loaded[row.parity], count_parity(16, row))
                if n == "q":
                    pe.wait_ge(nT_evac, count(NG, row, -NG - 1))
                    pe.wait_ge(raw_ready, count(2, row, 0))
                else:
                    pe.wait_ge(raw_ready, count(2, row, 1))
                nc.tensor.matmul(X[0][:], wq_s if n == "q" else wk_s, xT_s[row.parity][:],
                                 start=True, stop=True).then_inc(proj_ready, 1)

            def project_v(row):
                pe.wait_ge(nT_evac, count(NG, row, -NG + 2))
                if row.reg is None and row.n == 0:
                    pe.wait_ge(const_loaded, CONST)
                for t in range(NT):
                    mm = nc.tensor.matmul(X[1][:, P * t:P * (t + 1)], xT_s[row.parity][:, P * t:P * (t + 1)],
                                          wv_s, start=True, stop=True)
                mm.then_inc(v_ready, 1)

            def max_rows(b, g):
                dst = X[(1, 0, 1, 0)[g]]
                pe.wait_ge(nparts_ready, count(NG, b, g))
                pe.wait_ge(nT_evac, count(NG, b, g - 1))
                if g == 0:
                    pe.wait_ge(v_evac, count(1, b, 1))
                if g == 1:
                    pe.wait_ge(raw_ready, count(2, b + 1, 2))
                if g == 2:
                    pe.wait_ge(x1T_evac, count(1, b - 2, 1))
                if g == 3:
                    pe.wait_ge(gate_step, count(GATE, b - 2, 1))
                nc.tensor.transpose(dst[0:32, 0:P // 2].bitcast(BF16),
                                    nparts[(g - 1) % 2][:].rearrange("p r n -> p (r n)"),
                                    idb_s).then_inc(nT_ready, 1)

            def scores(b, g, u):
                if g == 0 and u == 0:
                    pe.wait_ge(stacked["q"][b.parity], count_parity(96, b))
                    pe.wait_ge(stacked["k"][b.parity], count_parity(96, b))
                qt, heads = score_unit(u)
                dst = S[(SU * g + u) % 2]
                pe.wait_ge(max_done, count(NG * SU, b, SU * g + u - 1))
                n = P * (qt + 1)
                for j, hg in enumerate(heads):
                    h, at = HG * g + hg, n * j
                    nc.tensor.matmul(dst[:, at:at + n], qs[b.parity][0:KS, h, P * qt:P * (qt + 1)],
                                     ks[b.parity][0:KS, h, 0:n], start=True, stop=False)
                    mm = nc.tensor.matmul(dst[:, at + n - P:at + n], idb_s, causal_s,
                                          start=False, stop=True)
                mm.then_inc(s_ready, 1)

            def key_scores(b, g, u):
                row, gg = (b, g - 2) if g >= 2 else (b - 1, g + 2)
                if u == 0:
                    pair = 16 * 2 * b.n + 16 * ((g - 2) // 2 + 1)
                    if b.reg is None:
                        pe.wait_ge(nrow_stacked[g % 2], pair)
                    else:
                        pe.wait_ge(nrow_stacked[g % 2], b.reg * 64 + pair)
                pe.wait_ge(exp_done, count(NG * TU, row, TU * gg + u - 1))
                for hg, kb, at in key_unit(u):
                    h, n = HG * gg + hg, T - P * kb
                    mm = nc.tensor.matmul(ST[u % 2][:, at:at + n],
                                          ks[row.parity][0:KST, h, P * kb:P * (kb + 1)],
                                          qs[row.parity][0:KST, h, P * kb:T], start=True, stop=True)
                mm.then_inc(st_ready, 1)

            def values(b, g, kb):
                row, gg = (b, 0) if g == 3 else (b - 1, g + 1)
                if kb == 0:
                    pe.wait_ge(y_evac, count(NG, row, gg))
                    pe.wait_ge(v_evac, count(1, row, 1))
                pe.wait_ge(masked, count(4 * NG, row, 4 * gg + (1, 3, 4, 4)[kb]))
                for hg in range(HG):
                    unit, at = key_place(hg, kb)
                    mm = nc.tensor.matmul(PV[32 * hg:32 * hg + 32, P * kb:T], vx[row.parity][:, kb, HG * gg + hg, :],
                                          prob[:, TU * (gg % 2) + unit, at:at + T - P * kb],
                                          start=(kb == 0), stop=(kb == NT - 1))
                mm.then_inc(pv_done, 1)

            def output(row):
                b = row + 2
                pe.wait_ge(yn_ready, count(1, row, 1))
                pe.wait_ge(nT_evac, count(NG, b, 0))
                pe.wait_ge(v_evac, count(1, b, 1))
                pe.wait_ge(x1T_evac, count(1, row, 0))
                for t in range(NT):
                    mm = nc.tensor.matmul(X[1][:, P * t:P * (t + 1)], yn[:, P * t:P * (t + 1)], wo_s,
                                          start=True, stop=True)
                mm.then_inc(o_ready, 1)

            def transpose_x1(row):
                pe.wait_ge(x1_ready, count(1, row, 1))
                for t in range(NT):
                    mm = nc.tensor.transpose(X[1][:, P * t:P * (t + 1)], x1[row.parity][:, t, :], id_s)
                mm.then_inc(x1T_ready, 1)

            def logits(row):
                b = row + 2
                pe.wait_ge(x1T_evac, count(1, row, 1))
                pe.wait_ge(nT_evac, count(NG, b, 1))
                pe.wait_ge(raw_ready, count(2, b + 1, 2))
                pe.wait_ge(gate_step, count(GATE, row - 1, 1))
                for c in range(NT):
                    mm = nc.tensor.matmul(X[0][32 * c:32 * c + 32, 0:P], wg_s, x1T[:, P * c:P * (c + 1)],
                                          start=True, stop=True)
                mm.then_inc(lg_ready, 1)

            def experts(row, k):
                if k == 0:
                    pe.wait_ge(ln2_step, count(LN, row, -LN + 1))
                    pe.wait_ge(gate_step, count(GATE, row, GATE))
                    nc.tensor.matmul(MO[:], wT[row.parity][:], be_s[:].rearrange("p t d -> p (t d)"),
                                     start=True, stop=False)
                else:
                    e, c = divmod(k - 1, NT)
                    if c == 0 and e < E_DVE:
                        pe.wait_ge(xs_dve, count(E_DVE, row, e + 1))
                    if c == 0 and e == E_DVE:
                        pe.wait_ge(xs_pool, count(1, row, 1))
                    mm = nc.tensor.matmul(MO[:, P * c:P * (c + 1)], xs[:, e, P * c:P * (c + 1)], we_s[:, e, :],
                                          start=False, stop=(k == EXPERT_PRODUCTS - 1))
                    if k == EXPERT_PRODUCTS - 1:
                        mm.then_inc(mo_ready, 1)

            def iteration(b):
                k = 0
                for g in range(NG):
                    for u in range(SU):
                        if g == 0 and u == 0 and (b + 1).real:
                            project("q", b + 1)
                        if g == 2 and u == 0 and (b - 2).real:
                            logits(b - 2)
                        if b.real:
                            scores(b, g, u)
                        if u < TU and group_real(b, g - 2):
                            key_scores(b, g, u)
                        if u == 3 and group_real(b, g - 1):
                            max_rows(b, g)
                        if u in (1, 4, 6, 8) and group_real(b, g - 3):
                            values(b, g, (1, 4, 6, 8).index(u))
                        if g == 0 and u == 5 and (b + 1).real:
                            project("k", b + 1)
                        if g == 0 and u == 7 and (b - 2).real:
                            output(b - 2)
                        if g == 1 and u == 5 and (b - 2).real:
                            transpose_x1(b - 2)
                        if g == 3 and u == 5 and (b + 1).real:
                            project_v(b + 1)
                        if (b - 3).real:
                            for _ in range((LATE_EXPERT_SLOTS if ending(b) else EXPERT_SLOTS).count((g, u))):
                                experts(b - 3, k)
                                k += 1

            pe.wait_ge(qk_loaded, QK_CONST)
            pipeline(pe, iteration)

        @block.scalar
        def _(act):
            def evac_raw(n, row):
                act.wait_ge(proj_ready, count(2, row, 1 + "qk".index(n)))
                act.wait_ge(rope_step[n], count(5, row, 0))
                act.wait_ge(swapped[n], count(32, row, 0))
                nc.scalar.activation(raw[n][:], X[0][:], ACT.Identity,
                                     bias=bq_s if n == "q" else bk_s).then_inc(raw_ready, 1)

            def part_hi(n, row):
                act.wait_ge(rope_step[n], count(5, row, 3))
                act.wait_ge(stacked[n][(row - 1).parity], count_parity(96, row - 1))
                nc.scalar.copy(parts[n][:, 0, :], rot[n][:]).then_inc(hi_ready[n], 1)

            def part_mid(n, row):
                act.wait_ge(rope_step[n], count(5, row, 4))
                nc.scalar.copy(parts[n][:, 1, :], rest[n][:]).then_inc(mid_ready[n], 1)

            def exponent(b, g, u):
                row, gg = (b, g - 2) if g >= 2 else (b - 1, g + 2)
                if u == 0:
                    act.wait_ge(pv_done, count(4 * NG, row, 4 * (gg - 1)))
                act.wait_ge(st_ready, count(NG * TU, row, TU * gg + u + 1))
                nc.scalar.activation(prob[:, TU * (gg % 2) + u, :], ST[u % 2][:], ACT.Exp,
                                     scale=SCALE).then_inc(exp_done, 1)

            def evac_max_rows(b, g):
                act.wait_ge(nT_ready, count(NG, b, g))
                if group_real(b, g - 3):
                    value = 16 * 2 * b.n + 16 * ((g - 3) // 2 + 1)
                    act.wait_ge(nrow_stacked[(g - 1) % 2], value if b.reg is None else b.reg * 64 + value)
                nc.scalar.copy(nrows[(g - 1) % 2][:], X[(1, 0, 1, 0)[g]][0:32, 0:P // 2].bitcast(BF16)
                               ).then_inc(nT_evac, 1)

            def evac_y(b, g):
                row, gg = (b, 0) if g == 3 else (b - 1, g + 1)
                act.wait_ge(pv_done, count(4 * NG, row, 4 * gg + 4))
                if group_real(row, gg - 2):
                    old = row if gg >= 2 else row - 1
                    act.wait_ge(y_moved[(gg - 2) % NG], count(16 * HG, old, 16 * HG))
                    act.wait_ge(den_moved[(gg - 2) % NG], count(16, old, 16))
                nc.scalar.copy(ysum[gg % 2][:], PV[:]).then_inc(y_evac, 1)

            def iteration(b):
                for g in range(NG):
                    for u in range(SU):
                        if u < TU and group_real(b, g - 2):
                            exponent(b, g, u)
                        if u == 5 and group_real(b, g - 1):
                            evac_max_rows(b, g)
                        if u == 10 and group_real(b, g - 3):
                            evac_y(b, g)
                        if (b + 1).real:
                            if (g, u) == (0, 1):
                                evac_raw("q", b + 1)
                            if (g, u) == (0, 6):
                                evac_raw("k", b + 1)
                            if (g, u) == (1, 1):
                                part_hi("q", b + 1)
                            if (g, u) == (1, 7):
                                part_mid("q", b + 1)
                            if (g, u) == (1, 10):
                                part_hi("k", b + 1)
                            if (g, u) == (2, 3):
                                part_mid("k", b + 1)
                        if (b - 2).real:
                            if (g, u) == (1, 7):
                                act.wait_ge(x1T_ready, count(1, b - 2, 1))
                                act.wait_ge(xs_dve, count(E_DVE, b - 2, 0))
                                act.wait_ge(xs_pool, count(1, b - 2, 0))
                                nc.scalar.copy(x1T[:], X[1][:]).then_inc(x1T_evac, 1)
                            if (g, u) == (2, 6):
                                act.wait_ge(gate_step, count(GATE, b - 2, 8))
                                nc.scalar.activation(gv[3][:], gv[2][:], ACT.Exp).then_inc(p2_ready, 1)

            act.wait_ge(qk_loaded, QK_CONST)
            pipeline(act, iteration)

        @block.vector
        def _(dve):
            def reduce_scores(b, g, u):
                qt, heads = score_unit(u)
                n = P * (qt + 1)
                dve.wait_ge(s_ready, count(NG * SU, b, SU * g + u + 1))
                nc.vector.tensor_reduce(nmax[g % 2][:, heads[0]:heads[-1] + 1, qt],
                                        S[(SU * g + u) % 2][:, 0:n * len(heads)].rearrange("p (h n) -> p h n", n=n),
                                        AX.X, ALU.max, negate=True).then_inc(max_done, 1)

            def split_max(b, g):
                dve.wait_ge(max_done, count(NG * SU, b, SU * (g + 1)))
                dve.wait_ge(nT_ready, count(NG, b, g - 1))
                m = nmax[g % 2][:].rearrange("p h t -> p (h t)")
                nc.vector.tensor_copy(nparts[g % 2][:, 0, :], m).then_inc(nhi_ready, 1)
                dve.wait_ge(nhi_ready, count(NG, b, g + 1))
                nc.vector.tensor_tensor(nparts[g % 2][:, 1, :], m, nparts[g % 2][:, 0, :],
                                        ALU.subtract).then_inc(nparts_ready, 1)

            def evac_v(row):
                dve.wait_ge(v_ready, count(1, row, 1))
                dve.wait_ge(pv_done, count(4 * NG, row, -4 * NG))
                nc.vector.tensor_tensor(vx[row.parity][:, :, :, 0:DH],
                                        X[1][:].rearrange("p (t h d) -> p t h d", t=NT, h=H),
                                        bv_s[:].rearrange("p (h d) -> p h d", h=H).unsqueeze(1)
                                        .to_broadcast((P, NT, H, DH)), ALU.add).then_inc(v_evac, 1)

            def invert_sums(row):
                for moved in den_moved:
                    dve.wait_ge(moved, count(16, row, 16))
                dve.wait_ge(rden_stored, count(16, row, -16))
                nc.vector.reciprocal(rden[row.parity][:], den[row.parity][:]).then_inc(rden_ready, 1)

            def norm(row, step, base, src, other, r, st, mv, rs_step, rs, dst, done, guard):
                sem_ = base
                if step == 0:
                    guard()
                    nc.vector.tensor_tensor(r[:], src[:].rearrange("p (t d) -> p t d", t=NT), other[:],
                                            ALU.add).then_inc(sem_, 1)
                if step == 1:
                    dve.wait_ge(sem_, count(LN, row, 1))
                    for t in range(NT):
                        ins = nc.vector.bn_stats(st[:, t, :], r[:, t, :])
                    ins.then_inc(sem_, 1)
                if step == 2:
                    dve.wait_ge(sem_, count(LN, row, 2))
                    dve.wait_ge(rs_step, count(2, row, 0))
                    dve.sem_inc(held["dve"])
                    for t in range(NT):
                        ins = nc.vector.bn_aggr(mv[:, t, :], st[:, t, :])
                    ins.then_inc(sem_, 1)
                if step == 3:
                    dve.wait_ge(rs_step, count(2, row, 2))
                    dve.wait_ge(sem_, count(LN, row, 3))
                    for t in range(NT):
                        ins = nc.vector.tensor_scalar(dst[:, t, :], r[:, t, :], mv[:, t, 0:1], rs[:, t:t + 1],
                                                      ALU.subtract, ALU.mult)
                    ins.then_inc(done, 1)

            def norm1(row, step):
                def guard():
                    dve.wait_ge(o_ready, count(1, row, 1))
                    dve.wait_ge(xb_ready, count(1, row, 1))
                if step == 3:
                    dve.wait_ge(x1T_ready, count(1, row, -1))
                    dve.wait_ge(ln2_step, count(LN, row, -LN - LN + 1))
                norm(row, step, ln1_step, X[1], xb, r1, st1, mv1, rs1_step, rs1, x1[row.parity], x1_ready, guard)

            def norm2(row, step):
                def guard():
                    dve.wait_ge(mo_ready, count(1, row, 1))
                if step == 3:
                    dve.wait_ge(stored, count(16, row, 0))
                norm(row, step, ln2_step, MO, x1[row.parity], r2, st2, mv2, rs2_step, rs2, x2,
                     x2_ready, guard)

            def gates_a(row):
                dve.wait_ge(lg_ready, count(1, row, 1))
                nc.vector.transpose(lg[:].rearrange("p a e -> p (a e)"), X[0][:, 0:P]).then_inc(gate_step, 1)
                dve.wait_ge(gate_step, count(GATE, row, 1))
                nc.vector.tensor_reduce(m1_, lg[:, :, 0:E], AX.X, ALU.max).then_inc(gate_step, 1)
                dve.wait_ge(gate_step, count(GATE, row, 2))
                nc.vector.tensor_tensor(gw[0][:], lg[:, :, 0:E], gv[0][:].to_broadcast((P, NT, E)),
                                        ALU.subtract).then_inc(gate_step, 1)

            def gates_b(row):
                dve.wait_ge(gate_step, count(GATE, row, 3))
                nc.vector.scalar_tensor_tensor(out=gw[1][:], in0=gw[0][:], scalar=0.0, in1=ramp_s[:],
                                               op0=ALU.is_ge, op1=ALU.mult).then_inc(gate_step, 1)
                dve.wait_ge(gate_step, count(GATE, row, 4))
                nc.vector.tensor_reduce(gv[1][:].rearrange("p t o -> p (t o)"), gw[1][:], AX.X, ALU.max).then_inc(gate_step, 1)
                dve.wait_ge(gate_step, count(GATE, row, 5))
                nc.vector.tensor_tensor(gw[2][:], gw[1][:], gv[1][:].to_broadcast((P, NT, E)),
                                        ALU.is_equal).then_inc(gate_step, 1)

            def gates_c(row):
                dve.wait_ge(gate_step, count(GATE, row, 6))
                nc.vector.scalar_tensor_tensor(out=gw[3][:], in0=gw[2][:], scalar=-1e38, in1=gw[0][:],
                                               op0=ALU.mult, op1=ALU.add).then_inc(gate_step, 1)
                dve.wait_ge(gate_step, count(GATE, row, 7))
                dve.wait_ge(p2_ready, count(1, row, 0))
                nc.vector.tensor_reduce(gv[2][:].rearrange("p t o -> p (t o)"), gw[3][:], AX.X, ALU.max).then_inc(gate_step, 1)

            def gates_d(row):
                dve.wait_ge(gate_step, count(GATE, row, 8))
                nc.vector.tensor_tensor(gw[4][:], gw[3][:], gv[2][:].to_broadcast((P, NT, E)),
                                        ALU.is_equal).then_inc(gate_step, 1)
                dve.wait_ge(gate_step, count(GATE, row, 9))
                nc.vector.tensor_tensor(gw[5][:], gw[4][:], ramp_s, ALU.mult).then_inc(gate_step, 1)
                dve.wait_ge(gate_step, count(GATE, row, 10))
                nc.vector.tensor_reduce(gv[4][:].rearrange("p t o -> p (t o)"), gw[5][:], AX.X, ALU.max).then_inc(gate_step, 1)
                dve.wait_ge(gate_step, count(GATE, row, 11))
                nc.vector.tensor_tensor(gw[6][:], gw[5][:], gv[4][:].to_broadcast((P, NT, E)),
                                        ALU.is_equal).then_inc(gate_step, 1)

            def gates_e(row):
                dve.wait_ge(p2_ready, count(1, row, 1))
                nc.vector.tensor_scalar(gv[5][:], gv[3][:], 1.0, None, ALU.add).then_inc(gate_step, 1)
                dve.wait_ge(gate_step, count(GATE, row, 13))
                nc.vector.reciprocal(gv[6][:], gv[5][:]).then_inc(gate_step, 1)
                dve.wait_ge(gate_step, count(GATE, row, 14))
                nc.vector.tensor_tensor(gv[7][:], gv[3][:], gv[6][:], ALU.mult).then_inc(gate_step, 1)

            def gates_f(row):
                nc.vector.tensor_tensor(gw[7][:], gw[2][:], gv[6][:].to_broadcast((P, NT, E)),
                                        ALU.mult).then_inc(gate_step, 1)
                dve.wait_ge(gate_step, count(GATE, row, 15))
                nc.vector.tensor_tensor(gw[8][:], gw[6][:], gv[7][:].to_broadcast((P, NT, E)),
                                        ALU.mult).then_inc(gate_step, 1)
                dve.wait_ge(gate_step, count(GATE, row, 17))
                nc.vector.tensor_tensor(wtok[:, :, 0:E], gw[7][:], gw[8][:], ALU.add).then_inc(gate_step, 1)
                dve.wait_ge(gate_step, count(GATE, row, 18))
                dve.wait_ge(w_stored, count(64, row, -64))
                dve.wait_ge(mo_ready, count(1, row, -1))
                nc.vector.transpose(wT[row.parity][:], wtok[:].rearrange("p a e -> p (a e)")).then_inc(gate_step, 1)

            m1_ = gv[0][:].rearrange("p t o -> p (t o)")

            def scale_x1(row, e):
                dve.wait_ge(wb_loaded[e // EH], count(16, row, 16))
                dve.wait_ge(x1T_evac, count(1, row, 1))
                nc.vector.tensor_tensor(xs[:, e, :], wb[:, e, :], x1T[:], ALU.mult).then_inc(xs_dve, 1)

            def iteration(b):
                for g in range(NG):
                    for u in range(SU):
                        if b.real:
                            reduce_scores(b, g, u)
                            if u == SU - 1:
                                split_max(b, g)
                        at = (g, u)
                        if (b - 2).real:
                            if at == (0, 9):
                                norm1(b - 2, 0)
                            if at == (0, 10):
                                norm1(b - 2, 1)
                            if at == (1, 0):
                                norm1(b - 2, 2)
                            if at == (1, 3):
                                norm1(b - 2, 3)
                            if at == (2, 1):
                                gates_a(b - 2)
                            if at == (2, 2):
                                gates_b(b - 2)
                            if at == (2, 3):
                                gates_c(b - 2)
                            if at == (2, 5):
                                gates_d(b - 2)
                            if at == (2, 7):
                                gates_e(b - 2)
                            if at == (2, 8):
                                gates_f(b - 2)
                        if (b - 3).real:
                            slots = LATE_SCALE_SLOTS if ending(b) else SCALE_SLOTS
                            if at in slots:
                                scale_x1(b - 3, slots.index(at))
                            if at == (3, 3):
                                norm2(b - 3, 0)
                            if at == (3, 4):
                                norm2(b - 3, 1)
                            if at == (3, 5):
                                norm2(b - 3, 2)
                            if at == (3, 10):
                                norm2(b - 3, 3)
                        if at == (3, 7) and (b + 1).real:
                            evac_v(b + 1)
                        if at == (3, 6) and (b - 1).real:
                            invert_sums(b - 1)

            nc.vector.memset(qs[0][0:KS, :, :], 0.0).then_inc(stack_set[0], 1)
            nc.vector.memset(ks[0][:], 1.0).then_inc(stack_set[0], 1)
            nc.vector.memset(wtok[:], 0.0).then_inc(wtok_set, 1)
            dve.wait_ge(qk_loaded, QK_CONST)
            dve.wait_ge(swapped["k"], 32)
            nc.vector.tensor_tensor(rot["k"][:], raw["k"][:], cos_s, ALU.mult).then_inc(rope_step["k"], 1)
            nc.vector.tensor_tensor(rest["k"][:], swap["k"][:], sin_s, ALU.mult).then_inc(rope_step["k"], 1)
            dve.wait_ge(rope_step["k"], 2)
            nc.vector.tensor_tensor(rot["k"][:], rot["k"][:], rest["k"][:], ALU.add).then_inc(rope_step["k"], 1)
            nc.vector.memset(qs[1][0:KS, :, :], 0.0).then_inc(stack_set[1], 1)
            dve.wait_ge(rope_step["k"], 3)
            dve.wait_ge(hi_ready["k"], 1)
            nc.vector.tensor_tensor(rest["k"][:], rot["k"][:], parts["k"][:, 0, :],
                                    ALU.subtract).then_inc(rope_step["k"], 1)
            dve.wait_ge(rope_step["k"], 4)
            dve.wait_ge(mid_ready["k"], 1)
            nc.vector.tensor_tensor(parts["k"][:, 2, :], rest["k"][:], parts["k"][:, 1, :],
                                    ALU.subtract).then_inc(rope_step["k"], 1)
            nc.vector.memset(ks[1][:], 1.0).then_inc(stack_set[1], 1)
            dve.wait_ge(const_loaded, CONST)
            dve.wait_ge(vx_set, 2)
            dve.wait_ge(wtok_set, 1)
            pipeline(dve, iteration)

        @block.gpsimd
        def _(pool):
            G_ = nc.gpsimd

            def rope(n, row, step):
                s = rope_step[n]
                if step == 0:
                    pool.wait_ge(swapped[n], count(32, row, 32))
                    G_.tensor_tensor(rot[n][:], raw[n][:], cos_s, ALU.mult).then_inc(s, 1)
                if step == 1:
                    G_.tensor_tensor(rest[n][:], swap[n][:], sin_s, ALU.mult).then_inc(s, 1)
                if step == 2:
                    pool.wait_ge(s, count(5, row, 2))
                    G_.tensor_tensor(rot[n][:], rot[n][:], rest[n][:], ALU.add).then_inc(s, 1)
                if step == 3:
                    pool.wait_ge(s, count(5, row, 3))
                    pool.wait_ge(hi_ready[n], count(1, row, 1))
                    G_.tensor_tensor(rest[n][:], rot[n][:], parts[n][:, 0, :], ALU.subtract).then_inc(s, 1)
                if step == 4:
                    pool.wait_ge(s, count(5, row, 4))
                    pool.wait_ge(mid_ready[n], count(1, row, 1))
                    G_.tensor_tensor(parts[n][:, 2, :], rest[n][:], parts[n][:, 1, :], ALU.subtract).then_inc(s, 1)

            def mask(b, g, k):
                row, gg = (b, g - 2) if g >= 2 else (b - 1, g + 2)
                pool.wait_ge(exp_done, count(NG * TU, row, TU * gg + (4, 6, 8, 10)[k]))
                pool.sem_inc(held["pool"])
                s = TU * (gg % 2)
                if k == 0:
                    v, pattern = prob[:, s:s + 4, 0:P], [[0, 4], [1, P]]
                elif k < 3:
                    v = prob[:, s + 2 + 2 * k:s + 4 + 2 * k, 0:2 * P]
                    pattern = [[0, 2], [0, 2], [1, P]]
                else:
                    v = prob[:, s + 8:s + 10, :].rearrange("p u (c q) -> p (u c) q", q=2 * P)[:, :, 0:P]
                    pattern = [[0, 4], [1, P]]
                G_.affine_select(out=v, in_=v, compare_op=ALU.is_ge, fill=0.0, base=0, pattern=pattern,
                                 channel_multiplier=-1).then_inc(masked, 1)

            def inverse_root(row, ln_step, rs_step, mv, ve, rs, used):
                pool.wait_ge(ln_step, count(LN, row, 3))
                pool.wait_ge(used, count(1, row, 0))
                pool.sem_inc(held["pool"])
                G_.tensor_scalar(ve[:], mv[:, :, 1], EPS, None, ALU.add).then_inc(rs_step, 1)
                pool.wait_ge(rs_step, count(2, row, 1))
                G_.tensor_tensor(rs[:], ve[:], half_s[:], ALU.pow).then_inc(rs_step, 1)

            def iteration(b):
                for g in range(NG):
                    for k in range(4):
                        at = (g, k)
                        if (b - 2).real:
                            row = b - 2
                            if at == (0, 0):
                                if row.reg is None and row.n == 0:
                                    pool.wait_ge(const_loaded, CONST)
                                pool.wait_ge(x_loaded[row.parity], count_parity(16, row))
                                pool.wait_ge(ln1_step, count(LN, row, -LN + 1))
                                G_.tensor_tensor(xb[:], x_s[row.parity][:],
                                                 bo_s[:].unsqueeze(1).to_broadcast((P, NT, P)), ALU.add
                                                 ).then_inc(xb_ready, 1)
                            if at == (0, 1):
                                for moved in y_moved:
                                    pool.wait_ge(moved, count(16 * HG, row, 16 * HG))
                                pool.wait_ge(rdenb_loaded, count(16, row, 16))
                                pool.wait_ge(o_ready, count(1, row, 0))
                                G_.tensor_tensor(yn[:], yT[row.parity][:], rdenb[:], ALU.mult).then_inc(yn_ready, 1)
                            if at == (1, 0):
                                inverse_root(row, ln1_step, rs1_step, mv1, ve1, rs1, x1_ready)
                        if (b - 3).real and at == ((1, 2) if ending(b) else (0, 2)):
                            pool.wait_ge(wb_loaded[1], count(16, b - 3, 16))
                            pool.wait_ge(x1T_evac, count(1, b - 3, 1))
                            G_.tensor_tensor(xs[:, E_DVE:E, :], wb[:, E_DVE:E, :],
                                             x1T[:].unsqueeze(1).to_broadcast((P, E - E_DVE, T)), ALU.mult
                                             ).then_inc(xs_pool, 1)
                        if (b - 3).real and at == (3, 3):
                            inverse_root(b - 3, ln2_step, rs2_step, mv2, ve2, rs2, x2_ready)
                        if (b + 1).real:
                            for when, n, step in ROPE_SLOTS:
                                if when == at and not (n == "k" and b.n == -1):
                                    rope(n, b + 1, step)
                        if group_real(b, g - 2):
                            mask(b, g, k)

            G_.memset(half_s[:], -0.5).then_inc(half_set, 1)
            for i in range(2):
                G_.memset(vx[i][:], 1.0).then_inc(vx_set, 1)
            pool.wait_ge(half_set, 1)
            pool.wait_ge(qk_loaded, QK_CONST)
            pipeline(pool, iteration)


GATE = 19
LN = 3
E_DVE = 6
SCALE_SLOTS = [(0, 1), (0, 2), (0, 3), (0, 4), (0, 6), (0, 8)]
EXPERT_SLOTS = [(0, u) for u in range(4, 11)] + [(1, u) for u in range(11)] + [(2, u) for u in range(11)]
EXPERT_SLOTS += [(3, 0), (3, 1), (1, 3), (2, 3)]
LATE_SCALE_SLOTS = [(1, u) for u in range(4, 4 + E_DVE)]
LATE_EXPERT_SLOTS = [(2, 1)] * EXPERT_PRODUCTS
ROPE_SLOTS = [((0, 1), "q", 0), ((0, 2), "q", 1), ((0, 3), "q", 2), ((1, 0), "k", 0), ((1, 1), "k", 1),
              ((1, 1), "q", 3), ((1, 2), "k", 2), ((1, 3), "q", 4), ((2, 0), "k", 3), ((2, 2), "k", 4)]


def kernel(**inputs):
    import concourse.bacc as bacc
    from concourse.bass_utils import run_bass_kernel_spmd as run

    a = {k: np.ascontiguousarray(v) for k, v in inputs.items()}
    x = a["L0_attn_x"].reshape(B * T, P)
    order = np.arange(P).reshape(H, DH).T.reshape(-1)
    f = np.float32
    theta = np.power(f(1250), f(-2.0) * np.arange(HALF, dtype=f) / f(DH)).astype(f)
    angle = np.arange(1, T + 1, dtype=f)[:, None] * np.concatenate([theta, theta])[None, :]
    cos_t = np.repeat(np.cos(angle).T, H, axis=0).astype(f)
    sign = np.where(np.arange(DH) < HALF, -1, 1).astype(f)
    sin_t = np.repeat((np.sin(angle) * sign).T, H, axis=0).astype(f)
    bf = mybir.dt.np(BF16)
    q, k = np.arange(P)[:, None], np.arange(P)[None, :]
    ident = np.eye(P, dtype=f)
    be = np.zeros((P, NT, P), f)
    for c in range(NT):
        be[32 * c:32 * c + E, c] = a["L0_ffn_be"]
    ramp = np.broadcast_to(E - np.arange(E, dtype=f), (P, NT, E)).reshape(P, NT * E)
    arrays = {
        "x": x, "xT": x.T,
        "qk_consts": np.hstack([a["L0_attn_Wq"].T[:, order], a["L0_attn_Wk"].T[:, order],
                                a["L0_attn_bq"][order].reshape(P, 1), a["L0_attn_bk"][order].reshape(P, 1)]),
        "rotation": np.stack([cos_t, sin_t], 1),
        "consts": np.hstack([a["L0_attn_Wv"].T, a["L0_attn_Wo"].T, ident, a["L0_ffn_Wg"],
                             np.zeros((P, 32 - E), f), ramp]),
        "masks": np.hstack([ident, np.where(k > q, f(-3e38), f(0))]).astype(bf),
        "bv": a["L0_attn_bv"].reshape(1, P), "bo": a["L0_attn_bo"].reshape(1, P),
        "we": a["L0_ffn_We"].transpose(1, 0, 2), "be": be,
    }
    nc = bacc.Bacc("TRN2", target_bir_lowering=False, num_devices=1)
    arrays = {n: np.ascontiguousarray(v) for n, v in arrays.items()}
    args = [nc.dram_tensor(n, v.shape, mybir.dt.from_np(v.dtype), kind="ExternalInput").ap() for n, v in arrays.items()]
    args.append(nc.dram_tensor("out", (B * T, P), F32, kind="ExternalOutput").ap())
    transformer_layer(nc, *args)
    r = run(nc, [arrays], core_ids=[0])
    return r.results[0]["out"].reshape(B, T, P)
```
